# Optimizing a Trainium2 kernel written in Bass

```python
import numpy as np
import jax
import jax.numpy as jnp

def _softmax(x, axis=-1):
    return jax.nn.softmax(x, axis=axis)

def _gelu(x):
    return jax.nn.gelu(x, approximate=True)

def _silu(x):
    return jax.nn.silu(x)

def _sigmoid(x):
    return jax.nn.sigmoid(x)

def _layernorm(x, axis=-1, eps=1e-05):
    m = jnp.mean(x, axis=axis, keepdims=True)
    v = jnp.var(x, axis=axis, keepdims=True)
    return (x - m) / jnp.sqrt(v + eps)

def _scatter_add(tgt, idx, src, axis=0):
    return tgt.at[idx].add(src)

def _segment_sum(src, seg, n):
    return jax.ops.segment_sum(src, seg, n)
kernel_name = 'mk_hybrid_d1_jaxref_r4_0cd301'

def setup_inputs(seed: int=0):
    np.random.seed(seed)
    _w = jnp.asarray

    def _L0_attn_a_setup():
        import jax, jax.numpy as jnp
        import numpy as np
        B, T, DIM, H = (2, 512, 256, 16)
        HD = DIM // H

        def _custom_softmax(a):
            a = jnp.clip(a, -100.0, 100.0)
            m = jnp.max(a, axis=-1, keepdims=True)
            e = jnp.exp(a - m)
            p = e / (jnp.sum(e, axis=-1, keepdims=True) + 1e-06)
            p = p + 1e-08
            return p / jnp.sum(p, axis=-1, keepdims=True)
        key = jax.random.key(seed)
        k1, k2, k3 = jax.random.split(key, 3)
        x = jax.random.normal(k1, (B, T, DIM), dtype=jnp.float32)
        w_qkv = jax.random.normal(k2, (3 * DIM, DIM), dtype=jnp.float32) / np.sqrt(DIM)
        w_proj = jax.random.normal(k3, (DIM, DIM), dtype=jnp.float32) / np.sqrt(DIM)
        return {'x': x, 'w_qkv': w_qkv, 'w_proj': w_proj}
    _L0_attn_a_in = _L0_attn_a_setup()

    def _L0_attn_b_setup():
        import jax, jax.numpy as jnp
        import numpy as np
        T, B, E = (256, 4, 256)
        H = 16
        D = E // H
        L = 16
        key = jax.random.key(seed)
        ks = jax.random.split(key, 4)
        query = jax.random.normal(ks[0], (T, B, E), dtype=jnp.float32)
        in_proj_weight = jax.random.normal(ks[1], (3 * E, E), dtype=jnp.float32) * (1.0 / np.sqrt(E))
        in_proj_bias = jnp.zeros((3 * E,), dtype=jnp.float32)
        rel_pos_keys = jax.random.normal(ks[2], (2 * L + 1, E), dtype=jnp.float32) * (1.0 / np.sqrt(E))
        out_w = jax.random.normal(ks[3], (E, E), dtype=jnp.float32) * (1.0 / np.sqrt(E))
        out_b = jnp.zeros((E,), dtype=jnp.float32)
        return {'query': query, 'in_proj_weight': in_proj_weight, 'in_proj_bias': in_proj_bias, 'rel_pos_keys': rel_pos_keys, 'out_w': out_w, 'out_b': out_b}
    _L0_attn_b_in = _L0_attn_b_setup()

    def _L0_ffn_setup():
        import jax, jax.numpy as jnp
        import numpy as np
        D_MODEL = 256
        N_HEAD = 16
        HEAD_DIM = D_MODEL // N_HEAD
        D_FF = 1024
        N_EXPERTS = 4
        EPS = 1e-05

        def _layer_norm(x, gamma, beta):
            mu = jnp.mean(x, axis=-1, keepdims=True)
            var = jnp.mean((x - mu) ** 2, axis=-1, keepdims=True)
            return (x - mu) / jnp.sqrt(var + EPS) * gamma + beta
        key = jax.random.key(seed)
        ks = jax.random.split(key, 20)
        f32 = jnp.float32
        sc = 1.0 / np.sqrt(D_MODEL)
        scf = 1.0 / np.sqrt(D_FF)
        return {'src': jax.random.normal(ks[0], (4, 128, D_MODEL), f32), 'Wq': jax.random.normal(ks[1], (D_MODEL, D_MODEL), f32) * sc, 'bq': jnp.zeros((D_MODEL,), f32), 'Wk': jax.random.normal(ks[2], (D_MODEL, D_MODEL), f32) * sc, 'bk': jnp.zeros((D_MODEL,), f32), 'Wv': jax.random.normal(ks[3], (D_MODEL, D_MODEL), f32) * sc, 'bv': jnp.zeros((D_MODEL,), f32), 'Wo': jax.random.normal(ks[4], (D_MODEL, D_MODEL), f32) * sc, 'bo': jnp.zeros((D_MODEL,), f32), 'router_w': jax.random.normal(ks[5], (D_MODEL, 1), f32) * 0.05, 'router_b': jnp.zeros((1,), f32), 'W1': jax.random.normal(ks[6], (N_EXPERTS, D_MODEL, D_FF), f32) * sc, 'b1': jnp.zeros((N_EXPERTS, D_FF), f32), 'W2': jax.random.normal(ks[7], (N_EXPERTS, D_FF, D_MODEL), f32) * scf, 'b2': jnp.zeros((N_EXPERTS, D_MODEL), f32), 'ln1_g': jnp.ones((D_MODEL,), f32), 'ln1_b': jnp.zeros((D_MODEL,), f32), 'ln2_g': jnp.ones((D_MODEL,), f32), 'ln2_b': jnp.zeros((D_MODEL,), f32)}
    _L0_ffn_in = _L0_ffn_setup()
    _d = {'L0_attn_a_x': _L0_attn_a_in['x'], 'L0_attn_a_w_qkv': _L0_attn_a_in['w_qkv'], 'L0_attn_a_w_proj': _L0_attn_a_in['w_proj'], 'L0_attn_b_in_proj_weight': _L0_attn_b_in['in_proj_weight'], 'L0_attn_b_in_proj_bias': _L0_attn_b_in['in_proj_bias'], 'L0_attn_b_rel_pos_keys': _L0_attn_b_in['rel_pos_keys'], 'L0_attn_b_out_w': _L0_attn_b_in['out_w'], 'L0_attn_b_out_b': _L0_attn_b_in['out_b'], 'L0_ffn_Wq': _L0_ffn_in['Wq'], 'L0_ffn_bq': _L0_ffn_in['bq'], 'L0_ffn_Wk': _L0_ffn_in['Wk'], 'L0_ffn_bk': _L0_ffn_in['bk'], 'L0_ffn_Wv': _L0_ffn_in['Wv'], 'L0_ffn_bv': _L0_ffn_in['bv'], 'L0_ffn_Wo': _L0_ffn_in['Wo'], 'L0_ffn_bo': _L0_ffn_in['bo'], 'L0_ffn_router_w': _L0_ffn_in['router_w'], 'L0_ffn_router_b': _L0_ffn_in['router_b'], 'L0_ffn_W1': _L0_ffn_in['W1'], 'L0_ffn_b1': _L0_ffn_in['b1'], 'L0_ffn_W2': _L0_ffn_in['W2'], 'L0_ffn_b2': _L0_ffn_in['b2'], 'L0_ffn_ln1_g': _L0_ffn_in['ln1_g'], 'L0_ffn_ln1_b': _L0_ffn_in['ln1_b'], 'L0_ffn_ln2_g': _L0_ffn_in['ln2_g'], 'L0_ffn_ln2_b': _L0_ffn_in['ln2_b']}
    _x0 = _d['L0_attn_a_x']
    _d['L0_attn_a_x'] = jax.random.normal(jax.random.fold_in(jax.random.key(seed), 1), (8, 512, 256), dtype=_x0.dtype)
    del _x0
    return _d

def reference(L0_attn_a_x, L0_attn_a_w_qkv, L0_attn_a_w_proj, L0_attn_b_in_proj_weight, L0_attn_b_in_proj_bias, L0_attn_b_rel_pos_keys, L0_attn_b_out_w, L0_attn_b_out_b, L0_ffn_Wq, L0_ffn_bq, L0_ffn_Wk, L0_ffn_bk, L0_ffn_Wv, L0_ffn_bv, L0_ffn_Wo, L0_ffn_bo, L0_ffn_router_w, L0_ffn_router_b, L0_ffn_W1, L0_ffn_b1, L0_ffn_W2, L0_ffn_b2, L0_ffn_ln1_g, L0_ffn_ln1_b, L0_ffn_ln2_g, L0_ffn_ln2_b):

    def _L0_attn_a_ref(x, w_qkv, w_proj):
        import jax, jax.numpy as jnp
        import numpy as np
        B, T, DIM, H = (2, 512, 256, 16)
        HD = DIM // H

        def _custom_softmax(a):
            a = jnp.clip(a, -100.0, 100.0)
            m = jnp.max(a, axis=-1, keepdims=True)
            e = jnp.exp(a - m)
            p = e / (jnp.sum(e, axis=-1, keepdims=True) + 1e-06)
            p = p + 1e-08
            return p / jnp.sum(p, axis=-1, keepdims=True)
        b, t, c = x.shape
        scale = HD ** (-0.5)
        qkv = jnp.einsum('btc,oc->bto', x, w_qkv)
        qkv = qkv.reshape(b, t, 3, H, HD)
        q = jnp.transpose(qkv[:, :, 0], (0, 2, 1, 3))
        k = jnp.transpose(qkv[:, :, 1], (0, 2, 1, 3))
        v = jnp.transpose(qkv[:, :, 2], (0, 2, 1, 3))
        attn = jnp.einsum('bhqd,bhkd->bhqk', q, k) * scale
        causal = jnp.tril(jnp.ones((t, t), dtype=bool))
        attn = jnp.where(causal, attn, -jnp.inf)
        attn = _custom_softmax(attn)
        out = jnp.einsum('bhqk,bhkd->bhqd', attn, v)
        out = jnp.transpose(out, (0, 2, 1, 3)).reshape(b, t, c)
        return jnp.einsum('btc,oc->bto', out, w_proj)

    def _L0_attn_b_ref(query, in_proj_weight, in_proj_bias, rel_pos_keys, out_w, out_b):
        import jax, jax.numpy as jnp
        import numpy as np
        T, B, E = (256, 4, 256)
        H = 16
        D = E // H
        L = 16
        t, b, e = query.shape
        scaling = D ** (-0.5)
        qkv = jnp.einsum('tbe,fe->tbf', query, in_proj_weight) + in_proj_bias
        q, k, v = jnp.split(qkv, 3, axis=-1)
        q = q * scaling

        def heads(x):
            return x.reshape(t, b * H, D).transpose(1, 0, 2)
        q, k, v = (heads(q), heads(k), heads(v))
        r = jnp.arange(t)
        dist = jnp.clip(r[None, :] - r[:, None], -L, L) + L
        rel_k = rel_pos_keys[dist][:, :, :D]
        scores = jnp.einsum('btd,bsd->bts', q, k) + jnp.einsum('btd,tsd->bts', q, rel_k)
        probs = jax.nn.softmax(scores, axis=-1)
        attn = jnp.einsum('bts,bsd->btd', probs, v)
        attn = attn.transpose(1, 0, 2).reshape(t, b, e)
        return jnp.einsum('tbe,oe->tbo', attn, out_w) + out_b

    def _L0_ffn_ref(src, Wq, bq, Wk, bk, Wv, bv, Wo, bo, router_w, router_b, W1, b1, W2, b2, ln1_g, ln1_b, ln2_g, ln2_b):
        import jax, jax.numpy as jnp
        import numpy as np
        D_MODEL = 256
        N_HEAD = 16
        HEAD_DIM = D_MODEL // N_HEAD
        D_FF = 1024
        N_EXPERTS = 4
        EPS = 1e-05

        def _layer_norm(x, gamma, beta):
            mu = jnp.mean(x, axis=-1, keepdims=True)
            var = jnp.mean((x - mu) ** 2, axis=-1, keepdims=True)
            return (x - mu) / jnp.sqrt(var + EPS) * gamma + beta
        B, T, _ = src.shape
        q = (src @ Wq + bq).reshape(B, T, N_HEAD, HEAD_DIM)
        k = (src @ Wk + bk).reshape(B, T, N_HEAD, HEAD_DIM)
        v = (src @ Wv + bv).reshape(B, T, N_HEAD, HEAD_DIM)
        scale = HEAD_DIM ** (-0.5)
        scores = jnp.einsum('bqhd,bkhd->bhqk', q, k) * scale
        probs = jax.nn.softmax(scores, axis=-1)
        attn = jnp.einsum('bhqk,bkhd->bqhd', probs, v).reshape(B, T, D_MODEL)
        attn = attn @ Wo + bo
        x = _layer_norm(src + attn, ln1_g, ln1_b)
        keys = (x @ router_w + router_b)[..., 0]
        expert_idx = jnp.remainder(jnp.floor(keys).astype(jnp.int32), N_EXPERTS)
        ff_out = jnp.zeros_like(x)
        for e in range(N_EXPERTS):
            h = jax.nn.relu(x @ W1[e] + b1[e])
            y = h @ W2[e] + b2[e]
            ff_out = ff_out + jnp.where((expert_idx == e)[..., None], y, 0.0)
        return _layer_norm(x + ff_out, ln2_g, ln2_b)
    x = L0_attn_a_x
    x = x + _L0_attn_a_ref(_layernorm(x, axis=-1), L0_attn_a_w_qkv, L0_attn_a_w_proj)
    x = x + _L0_ffn_ref(_layernorm(x, axis=-1), L0_ffn_Wq, L0_ffn_bq, L0_ffn_Wk, L0_ffn_bk, L0_ffn_Wv, L0_ffn_bv, L0_ffn_Wo, L0_ffn_bo, L0_ffn_router_w, L0_ffn_router_b, L0_ffn_W1, L0_ffn_b1, L0_ffn_W2, L0_ffn_b2, L0_ffn_ln1_g, L0_ffn_ln1_b, L0_ffn_ln2_g, L0_ffn_ln2_b)
    x = x + _L0_attn_b_ref(_layernorm(x, axis=-1), L0_attn_b_in_proj_weight, L0_attn_b_in_proj_bias, L0_attn_b_rel_pos_keys, L0_attn_b_out_w, L0_attn_b_out_b)
    x = x + _L0_ffn_ref(_layernorm(x, axis=-1), L0_ffn_Wq, L0_ffn_bq, L0_ffn_Wk, L0_ffn_bk, L0_ffn_Wv, L0_ffn_bv, L0_ffn_Wo, L0_ffn_bo, L0_ffn_router_w, L0_ffn_router_b, L0_ffn_W1, L0_ffn_b1, L0_ffn_W2, L0_ffn_b2, L0_ffn_ln1_g, L0_ffn_ln1_b, L0_ffn_ln2_g, L0_ffn_ln2_b)
    return x

_drawn_inputs = setup_inputs


def setup_inputs(seed=0):
    import zlib

    import numpy as np

    out = dict(_drawn_inputs(seed))
    spreads = {'L0_attn_b_in_proj_bias': (0.0, 0.1),
     'L0_attn_b_out_b': (0.0, 0.1),
     'L0_ffn_bq': (0.0, 0.1),
     'L0_ffn_bk': (0.0, 0.1),
     'L0_ffn_bv': (0.0, 0.1),
     'L0_ffn_bo': (0.0, 0.1),
     'L0_ffn_b1': (0.0, 0.1),
     'L0_ffn_b2': (0.0, 0.1),
     'L0_ffn_ln1_g': (1.0, 0.2),
     'L0_ffn_ln1_b': (0.0, 0.1),
     'L0_ffn_ln2_g': (1.0, 0.2),
     'L0_ffn_ln2_b': (0.0, 0.1)}
    factors = {}
    for name, (base, spread) in spreads.items():
        noise = np.random.default_rng([zlib.crc32(name.encode()), seed]).standard_normal(out[name].shape)
        drawn = base * np.exp(spread * noise) if base else spread * noise
        out[name] = jnp.asarray(drawn.astype(out[name].dtype))
    for name, factor in factors.items():
        out[name] = (out[name] * factor).astype(out[name].dtype)
    return out
```

```python
from contextlib import ExitStack

import concourse.bass as bass
from concourse import mybir

ALU = mybir.AluOpType
ACT = mybir.ActivationFunctionType
AX = mybir.AxisListType
F32 = mybir.dt.float32
BF16 = mybir.dt.bfloat16
I32 = mybir.dt.int32

P = 128
NB, T, D = 8, 512, 256
H, HD = 16, 16
NG = H // 4
KT = T // P
DC = D // P
NT = NB * KT
F, NE = 1024, 4
FC = F // P
EPS = 1e-5
SCALE = HD ** -0.5
MASKED = -1e30

Q_BLOCKS = (0, 1, 2, 0, 1, 0)
K_BLOCKS = (0, 0, 0, 1, 1, 2)


class Names:
    pass


class Layer:

    def __init__(self, base, t_base, src_base, causal, ffn, x_src, x_dst, w_qkv, w_o, b_qk, b_v, b_o):
        self.base, self.t_base, self.src_base = base, t_base, src_base
        self.causal, self.ffn = causal, ffn
        self.x_src, self.x_dst = x_src, x_dst
        self.w_qkv, self.w_o, self.b_qk, self.b_v, self.b_o = w_qkv, w_o, b_qk, b_v, b_o



def group_ahead(b, g, by):
    return (b, g + by) if g + by < NG else (b + 1, g + by - NG)


def attention(nc, M, S, C, ph):
    base = ph.base
    causal = ph.causal
    tb = ph.t_base
    UT = 20 if causal else 16
    FL = UT - 16

    def seq(b):
        return base + b

    def s_unit(b, g, i, qt):
        return 16 * (NG * seq(b) + g) + 4 * i + qt

    def t_unit(b, g, u):
        return tb + UT * (NG * b + g) + u

    def pv_count(b, g, kt):
        return NG * KT * seq(b) + KT * g + kt + 1

    def exists(b):
        return not (isinstance(b, int) and not 0 <= b < NB)

    USES = [((0, 0), "xnT", 1, 0), ((0, 0), "xnT", 1, 1),
            ((0, 1), "out", -1, 3), ((0, 1), "max", 0, 1),
            ((0, 2), "qk", 1, 0), ((0, 2), "qk", 1, 1),
            ((0, 3), "attT", -1, 0), ((0, 3), "attT", -1, 1),
            ((1, 0), "qk", 1, 2), ((1, 0), "qk", 1, 3),
            ((1, 1), "max", 0, 2), ((1, 1), "out", 0, 0),
            ((1, 2), "v", 1, 0), ((1, 2), "v", 1, 1),
            ((1, 3), "y", -1, 0), ((1, 3), "y", -1, 1),
            ((2, 1), "max", 0, 3), ((2, 1), "out", 0, 1),
            ((3, 1), "max", 1, 0), ((3, 1), "out", 0, 2)]
    READ_OUT = {"xnT": (2, S.xnT_ready), "max": (4, S.max_sb), "out": (4, S.att_ready), "qk": (4, S.qkf_ready),
                "attT": (2, S.attT_ready), "v": (2, S.v_sb), "y": (2, S.y_sb)}

    def bank_free(pe, at, b):
        body, p = b, at - 2
        while True:
            if p < 0:
                body, p = body - 1, p + len(USES)
            if isinstance(body, int) and body < -1:
                return
            _, what, off, idx = USES[p]
            n = body + off
            if exists(n):
                per, sem = READ_OUT[what]
                pe.wait_ge(sem, per * seq(n) + idx + 1)
                return
            p -= 2

    def uses(slot, b):
        return [(p, what, b + off, idx) for p, (sl, what, off, idx) in enumerate(USES)
                if sl == slot and exists(b + off)]

    def bodies(eng, body):
        body(0)
        with eng.Fori(1, NB - 2, 1) as b:
            body(b)
        body(NB - 2)
        body(NB - 1)

    block_of = nc.Block()
    with block_of as block:

        @block.sync
        def _(sp):
            def load_x(b):
                if not exists(b):
                    return
                if base or not isinstance(b, int) or b > 0:
                    sp.wait_ge(S.xn_ready, seq(b))
                sp.dma_start(M.x_in[:, :, :], ph.x_src[b].rearrange("(t p) d -> p t d", p=P)).then_inc(S.x_loaded, 16)

            def write_parts(b, half):
                for isk in (0, 1):
                    j = 2 * half + isk
                    sp.wait_ge(S.split_step, 3 * (4 * seq(b) + j + 1))
                    if isk == 0:
                        for p in range(3):
                            sp.dma_start(M.q_parts_d[b][8 * half:8 * half + 8, HD * p:HD * p + HD, :],
                                         M.parts[:, j, p, :]).then_inc(S.parts_written[half], 16)
                    else:
                        for blk, p in enumerate(K_BLOCKS):
                            sp.dma_start(M.k_parts_d[b][8 * half:8 * half + 8, HD * blk:HD * blk + HD, :],
                                         M.parts[:, j, p, :]).then_inc(S.parts_written[half], 16)

            def load_stack(b, g):
                half = g // 2
                sp.wait_ge(S.parts_written[half], 144 * (seq(b) + 1))
                if not isinstance(b, int) or b > 0:
                    sp.wait_ge(S.t_ps, t_unit(b - 1, g, UT))
                hs = slice(4 * g, 4 * g + 4)
                for row, rows in ((0, 48), (48, 32), (80, 16)):
                    sp.dma_start(M.stack_q[row:row + rows, g, :, :],
                                 M.q_parts_d[b][hs, 0:rows, :].rearrange("h r t -> r h t")).then_inc(S.stack_loaded[g], 16)
                sp.dma_start(M.stack_k[0:96, g, :, :],
                             M.k_parts_d[b][hs, :, :].rearrange("h r t -> r h t")).then_inc(S.stack_loaded[g], 16)

            def load_max_rows(b, g):
                sp.wait_ge(S.max_sb, NG * seq(b) + g + 1)
                sp.dma_start(M.stack_q[96:99, g, :, :], M.max_sb[:, g % 2, :]).then_inc(S.max_rows[g], 16)

            def load_res(b):
                if not exists(b):
                    return
                if ph.ffn:
                    sp.wait_ge(S.src_saved, 16 * (ph.src_base + b + 1))
                    src = M.src_d[b]
                else:
                    src = ph.x_src[b]
                if base or not isinstance(b, int) or b > 0:
                    sp.wait_ge(S.y_sb, 2 * seq(b))
                sp.dma_start(M.res[:, :, :], src.rearrange("(t p) d -> p t d", p=P)).then_inc(S.res_loaded, 16)

            def save_src(b):
                if not (exists(b) and ph.ffn):
                    return
                sp.wait_ge(S.xn_ready, seq(b) + 1)
                sp.dma_start(M.src_d[b].rearrange("(t p) d -> p t d", p=P), M.xn[:, :, :]).then_inc(S.src_saved, 16)

            def store(b):
                if not exists(b):
                    return
                if ph.ffn:
                    sp.wait_ge(S.x1_ready, ph.src_base + b + 1)
                else:
                    sp.wait_ge(S.y_sb, 2 * seq(b) + 2)
                sp.dma_start(ph.x_dst[b].rearrange("(t p) d -> p t d", p=P), M.x_out[:, :, :]).then_inc(S.x_stored, 16)

            def body(b):
                if not (isinstance(b, int) and b == 0):
                    load_stack(b, 3)
                load_x(b + 2)
                load_res(b - 1)
                load_max_rows(b, 1)
                if exists(b + 1):
                    write_parts(b + 1, 0)
                load_max_rows(b, 2)
                if exists(b + 1):
                    load_stack(b + 1, 0)
                    write_parts(b + 1, 1)
                    load_stack(b + 1, 1)
                load_max_rows(b, 3)
                store(b - 1)
                if exists(b + 1):
                    load_stack(b + 1, 2)
                    load_max_rows(b + 1, 0)
                save_src(b + 2)

            load_x(0)
            save_src(0)
            load_x(1)
            write_parts(0, 0)
            load_stack(0, 0)
            load_stack(0, 1)
            write_parts(0, 1)
            load_stack(0, 2)
            load_stack(0, 3)
            load_max_rows(0, 0)
            save_src(1)
            bodies(sp, body)
            load_res(NB - 1)
            store(NB - 1)
            sp.wait_ge(S.x_stored, 16 * (base + NB))
            if ph.ffn:
                sp.wait_ge(S.src_saved, 16 * (ph.src_base + NB))

        @block.tensor
        def _(pe):
            def use_bank(at, what, b, idx, body_b):
                G = M.gen[at % 2]
                bank_free(pe, at, body_b)
                if what == "xnT":
                    pe.wait_ge(S.xn_ready, seq(b) + 1)
                    for t in range(KT):
                        last = nc.tensor.transpose(G[:, t * P:t * P + P], M.xn[:, t, idx * P:idx * P + P], C.ident[:, :])
                    last.then_inc(S.xnT_ps, 1)
                elif what == "qk":
                    half, isk = divmod(idx, 2)
                    pe.wait_ge(S.xnT_ready, 2 * seq(b) + 2)
                    o = D * isk + P * half
                    for c in range(DC):
                        last = nc.tensor.matmul(G[:, :], ph.w_qkv[:, c, o:o + P], M.xnT[:, c, :], start=(c == 0), stop=(c == DC - 1))
                    last.then_inc(S.qk_ps, 1)
                elif what == "v":
                    for t in (2 * idx, 2 * idx + 1):
                        for c in range(DC):
                            last = nc.tensor.matmul(G[:, (t % 2) * D:(t % 2) * D + D], M.xnT[:, c, t * P:t * P + P],
                                                    ph.w_qkv[:, c, 2 * D:3 * D], start=(c == 0), stop=(c == DC - 1))
                    last.then_inc(S.v_ps, 1)
                elif what == "max":
                    pe.wait_ge(S.max_split, 4 * (NG * seq(b) + idx + 1))
                    Gb = M.gen_bf[at % 2]
                    for t in range(KT):
                        last = nc.tensor.transpose(Gb[0:12, t * P:t * P + P], M.max_parts[:, t, :, :].rearrange("p a h -> p (a h)"), C.ident_bf[:, :])
                    if causal and idx == 1:
                        pe.wait_ge(S.v_total, seq(b) + 1)
                        last = nc.tensor.matmul(G[:, D:2 * D], C.ones[:, :], M.v_tot[:, :], start=True, stop=True)
                    last.then_inc(S.max_ps, 1)
                elif what == "out":
                    pe.wait_ge(S.o_sb, NG * seq(b) + idx + 1)
                    for t in range(KT):
                        last = nc.tensor.transpose(G[:, t * P:t * P + P], M.o_sb[:, t * P:t * P + P], C.ident[:, :])
                    last.then_inc(S.out_ps, 1)
                elif what == "attT":
                    pe.wait_ge(S.att_ready, NG * seq(b) + NG)
                    for t in range(KT):
                        last = nc.tensor.transpose(G[:, t * P:t * P + P], M.att[:, t, idx * P:idx * P + P], C.ident[:, :])
                    last.then_inc(S.attT_ps, 1)
                elif what == "y":
                    pe.wait_ge(S.attT_ready, 2 * seq(b) + 2)
                    for t in (2 * idx, 2 * idx + 1):
                        for c in range(DC):
                            last = nc.tensor.matmul(G[:, (t % 2) * D:(t % 2) * D + D], M.attT[:, c, t * P:t * P + P],
                                                    ph.w_o[:, c, :], start=(c == 0), stop=(c == DC - 1))
                    last.then_inc(S.y_ps, 1)

            def score(b, g, i, qt):
                if qt == 0 and i == 0:
                    pe.wait_ge(S.stack_loaded[g], 64 * (seq(b) + 1))
                u = s_unit(b, g, i, qt)
                if not (isinstance(u, int) and u < 2):
                    pe.wait_ge(S.max_done, u - 1)
                bank = M.sc[qt % 2]
                n = P * (qt + 1) if causal else T
                last = nc.tensor.matmul(bank[:, 0:n], M.stack_q[0:96, g, i, qt * P:qt * P + P], M.stack_k[0:96, g, i, 0:n],
                                        start=True, stop=True)
                if causal:
                    last = nc.tensor.matmul(bank[:, qt * P:qt * P + P], C.ident_bf[:, :], C.mask_qk[:, :],
                                            start=False, stop=True, skip_group_check=True)
                last.then_inc(S.sc_ps, 1)

            def score_t(b, g, kt, i):
                if kt == 0 and i == 0 and not causal:
                    pe.wait_ge(S.max_rows[g], 16 * (seq(b) + 1))
                u = t_unit(b, g, FL + 4 * kt + i)
                if not (isinstance(u, int) and u < 2):
                    pe.wait_ge(S.exp_done, u - 1)
                bank = M.sct[i % 2]
                q0 = kt * P if causal else 0
                last = nc.tensor.matmul(bank[:, 0:T - q0], M.stack_k[0:99, g, i, kt * P:kt * P + P], M.stack_q[0:99, g, i, q0:T],
                                        start=True, stop=True)
                if causal:
                    last = nc.tensor.matmul(bank[:, 0:P], C.ident_bf[:, :], C.mask_kq[:, :],
                                            start=False, stop=True, skip_group_check=True)
                last.then_inc(S.t_ps, 1)

            def floor_row(b, g, i):
                if i == 0:
                    pe.wait_ge(S.max_rows[g], 16 * (seq(b) + 1))
                u = t_unit(b, g, i)
                if not (isinstance(u, int) and u < 2):
                    pe.wait_ge(S.exp_done, u - 1)
                nc.tensor.matmul(M.sct[i % 2][:, :], M.stack_k[96:99, g, i, 0:P], M.stack_q[96:99, g, i, :],
                                 start=True, stop=True).then_inc(S.t_ps, 1)

            def pv(b, g, kt):
                if kt == 0:
                    pe.wait_ge(S.v_aug, NG * seq(b) + g + 1)
                    if base or not isinstance(b, int) or b > 0 or g >= 2:
                        pe.wait_ge(S.o_sb, NG * seq(b) + g - 1)
                q0 = kt * P if causal else 0
                bank = M.out[g % 2]
                end = kt == KT - 1
                for i in range(4):
                    if causal:
                        pe.wait_ge(S.clip_done, 16 * (NG * b + g) + 4 * kt + i + 1)
                    else:
                        pe.wait_ge(S.exp_done, t_unit(b, g, FL + 4 * kt + i) + 1)
                    last = nc.tensor.matmul(bank[32 * i:32 * i + 32, q0:T], M.v_aug[:, kt, 4 * g + i, :],
                                            M.prob[:, kt % 2, i, 0:T - q0], start=(kt == 0), stop=(kt == 0 if causal else end),
                                            skip_group_check=causal and kt > 0)
                if causal and end:
                    for t in range(KT - 1):
                        v = M.v_later[:, t] if t < KT - 2 else M.v_aug[:, KT - 1]
                        for i in range(4):
                            last = nc.tensor.matmul(bank[32 * i:32 * i + 32, t * P:t * P + P], v[:, 4 * g + i, :],
                                                    M.floor[:, g % 2, i, t * P:t * P + P], start=False, stop=(t == KT - 2),
                                                    skip_group_check=True)
                last.then_inc(S.pv_done, 1)

            def body(b):
                for g in range(NG):
                    sb, sg = group_ahead(b, g, 2)
                    for kt in range(KT):
                        if kt == 0 and causal:
                            for i in range(4):
                                floor_row(b, g, i)
                        for i in range(4):
                            score_t(b, g, kt, i)
                            if exists(sb):
                                score(sb, sg, kt, i)
                        for at, what, n, idx in uses((g, kt), b):
                            use_bank(at, what, n, idx, b)
                        if kt > 0:
                            pv(b, g, kt - 1)
                        elif g > 0:
                            pv(b, g - 1, KT - 1)
                        elif exists(b - 1):
                            pv(b - 1, NG - 1, KT - 1)

            for at, (_, what, off, idx) in enumerate(USES):
                if off == 1 and what != "max":
                    use_bank(at, what, 0, idx, -1)
            for g in (0, 1):
                for i in range(4):
                    for qt in range(KT):
                        score(0, g, i, qt)
                if g == 0:
                    use_bank(18, "max", 0, 0, -1)
            bodies(pe, body)
            pv(NB - 1, NG - 1, KT - 1)
            for at, (_, what, off, idx) in enumerate(USES):
                if off == -1:
                    use_bank(at, what, NB - 1, idx, NB)

        @block.scalar
        def _(act):
            def read_bank(at, what, b, idx):
                G = M.gen[at % 2]
                if what == "xnT":
                    act.wait_ge(S.xnT_ps, 2 * seq(b) + idx + 1)
                    if base or not isinstance(b, int) or b > 0:
                        act.wait_ge(S.v_ps, 2 * seq(b))
                    nc.scalar.activation(M.xnT[:, idx, :], G[:, :], ACT.Copy).then_inc(S.xnT_ready, 1)
                elif what == "qk":
                    half, isk = divmod(idx, 2)
                    act.wait_ge(S.qk_ps, 4 * seq(b) + idx + 1)
                    if base or not isinstance(b, int) or b > 0:
                        act.wait_ge(S.split_step, 3 * (4 * (seq(b) - 1) + idx + 1))
                    for dst in (M.qkf[:, idx, :], M.parts[:, idx, 0, :]):
                        if dst.dtype == BF16 and (base or not isinstance(b, int) or b > 0):
                            act.wait_ge(S.parts_written[half], 144 * seq(b))
                        last = nc.scalar.activation(dst, G[:, :], ACT.Identity, bias=ph.b_qk[:, idx:idx + 1],
                                                    scale=1.0 if isk else SCALE)
                    last.then_inc(S.qkf_ready, 1)
                elif what == "attT":
                    act.wait_ge(S.attT_ps, 2 * seq(b) + idx + 1)
                    if base or not isinstance(b, int) or b > 0:
                        act.wait_ge(S.y_ps, 2 * seq(b))
                    nc.scalar.activation(M.attT[:, idx, :], G[:, :], ACT.Copy).then_inc(S.attT_ready, 1)

            def read_out(b, g):
                act.wait_ge(S.pv_done, pv_count(b, g, KT - 1))
                if base or not isinstance(b, int) or b > 0 or g > 0:
                    act.wait_ge(S.out_ps, NG * seq(b) + g)
                nc.scalar.activation(M.o_sb[:, :], M.out[g % 2][:, :], ACT.Copy).then_inc(S.o_sb, 1)

            def exp(b, g, kt, i):
                u = t_unit(b, g, FL + 4 * kt + i)
                act.wait_ge(S.t_ps, u + 1)
                if kt >= 2:
                    act.wait_ge(S.pv_done, pv_count(b, g, kt - 2))
                elif base or not isinstance(b, int) or b > 0 or g > 0:
                    act.wait_ge(S.pv_done, pv_count(b, g, 0) + kt - 2)
                n = T - kt * P if causal else T
                nc.scalar.activation(M.prob[:, kt % 2, i, 0:n], M.sct[i % 2][:, 0:n], ACT.Exp).then_inc(S.exp_done, 1)

            def floor_exp(b, g, i):
                act.wait_ge(S.t_ps, t_unit(b, g, i) + 1)
                if not isinstance(b, int) or b > 0 or g > 1:
                    act.wait_ge(S.pv_done, pv_count(b, g, 0) - 1 - KT)
                nc.scalar.activation(M.floor[:, g % 2, i, :], M.sct[i % 2][:, :], ACT.Exp, bias=C.minus100[:, 0:1]).then_inc(S.exp_done, 1)

            def body(b):
                for g in range(NG):
                    for kt in range(KT):
                        if kt == 0 and causal:
                            for i in range(4):
                                floor_exp(b, g, i)
                        for i in range(4):
                            exp(b, g, kt, i)
                        for at, what, n, idx in uses((g, kt), b):
                            read_bank(at, what, n, idx)
                        if kt == 0:
                            if g > 0:
                                read_out(b, g - 1)
                            elif exists(b - 1):
                                read_out(b - 1, NG - 1)

            for at, (_, what, off, idx) in enumerate(USES):
                if off == 1 and what != "max":
                    read_bank(at, what, 0, idx)
            bodies(act, body)
            read_out(NB - 1, NG - 1)
            for at, (_, what, off, idx) in enumerate(USES):
                if off == -1:
                    read_bank(at, what, NB - 1, idx)

        @block.vector
        def _(dve):
            def row_max(b, g, i, qt):
                dve.wait_ge(S.sc_ps, s_unit(b, g, i, qt) + 1)
                n = P * (qt + 1) if causal else T
                nc.vector.tensor_reduce(M.neg_max[:, qt, i:i + 1], M.sc[qt % 2][:, 0:n], AX.X, ALU.max,
                                        negate=True).then_inc(S.max_done, 1)

            def split_max(b, g):
                dve.wait_ge(S.max_done, s_unit(b, g, 3, 3) + 1)
                if causal:
                    nc.vector.tensor_scalar(M.neg_max[:, :, :], M.neg_max[:, :, :], -100.0, 100.0, ALU.max, ALU.min).then_inc(S.max_clip, 1)
                    dve.wait_ge(S.max_clip, NG * b + g + 1)
                if base or not isinstance(b, int) or b > 0 or g > 0:
                    dve.wait_ge(S.max_ps, NG * seq(b) + g)
                st = 4 * (NG * seq(b) + g)
                nc.vector.tensor_copy(M.max_parts[:, :, 0, :], M.neg_max[:, :, :]).then_inc(S.max_split, 1)
                dve.wait_ge(S.max_split, st + 1)
                nc.vector.tensor_tensor(M.max_rest[:, :, :], M.neg_max[:, :, :], M.max_parts[:, :, 0, :], ALU.subtract).then_inc(S.max_split, 1)
                dve.wait_ge(S.max_split, st + 2)
                nc.vector.tensor_copy(M.max_parts[:, :, 1, :], M.max_rest[:, :, :]).then_inc(S.max_split, 1)
                dve.wait_ge(S.max_split, st + 3)
                nc.vector.tensor_tensor(M.max_parts[:, :, 2, :], M.max_rest[:, :, :], M.max_parts[:, :, 1, :], ALU.subtract).then_inc(S.max_split, 1)

            def clip(b, g, kt, i):
                dve.wait_ge(S.exp_done, t_unit(b, g, FL + 4 * kt + i) + 1)
                p = M.prob[:, kt % 2, i, 0:T - kt * P]
                nc.vector.scalar_tensor_tensor(out=p, in0=p, scalar=1.0, in1=M.floor[:, g % 2, i, kt * P:T],
                                               op0=ALU.min, op1=ALU.max).then_inc(S.clip_done, 1)

            def read_bank(at, what, b, idx):
                G = M.gen[at % 2]
                if what == "max":
                    dve.wait_ge(S.max_ps, NG * seq(b) + idx + 1)
                    if causal and idx == 1:
                        nc.vector.tensor_copy(M.v_all[:, :], G[:, D:2 * D]).then_inc(S.v_all, 1)
                    if base or not isinstance(b, int) or b > 0 or idx >= 2:
                        pb, pg = (b, idx - 2) if idx >= 2 else (b - 1, idx + 2)
                        dve.wait_ge(S.max_rows[pg], 16 * (seq(pb) + 1))
                    nc.vector.tensor_copy(M.max_sb[:, idx % 2, :], M.gen_bf[at % 2][0:12, 0:T]).then_inc(S.max_sb, 1)
                elif what == "v":
                    dve.wait_ge(S.v_ps, 2 * seq(b) + idx + 1)
                    if base or not isinstance(b, int) or b > 0:
                        dve.wait_ge(S.v_aug, NG * seq(b))
                        if causal:
                            dve.wait_ge(S.v_total, seq(b))
                    dst = M.v_st[:, 2 * idx:2 * idx + 2, :]
                    src = G[:, :].rearrange("p (t d) -> p t d", t=2)
                    if ph.b_v is None:
                        nc.vector.tensor_copy(dst, src).then_inc(S.v_sb, 1)
                    else:
                        nc.vector.tensor_tensor(dst, src, ph.b_v[:, :].unsqueeze(1).to_broadcast([P, 2, D]), ALU.add).then_inc(S.v_sb, 1)
                elif what == "out":
                    normalise(G, b, idx)
                elif what == "y":
                    dve.wait_ge(S.y_ps, 2 * seq(b) + idx + 1)
                    dst = M.tmp if ph.ffn else M.x_out
                    if idx == 0:
                        if ph.ffn:
                            dve.wait_ge(S.res_biased, ph.src_base + b + 1)
                            if ph.src_base or not isinstance(b, int) or b > 0:
                                dve.wait_ge(S.x1_ready, ph.src_base + b)
                        else:
                            dve.wait_ge(S.res_loaded, 16 * (seq(b) + 1))
                            if not isinstance(b, int) or b > 0:
                                dve.wait_ge(S.x_stored, 16 * seq(b))
                    nc.vector.tensor_tensor(dst[:, 2 * idx:2 * idx + 2, :], G[:, :].rearrange("p (t d) -> p t d", t=2),
                                            M.res[:, 2 * idx:2 * idx + 2, :], ALU.add).then_inc(S.y_sb, 1)
                    if idx == 1 and ph.ffn:
                        dve.wait_ge(S.y_sb, 2 * seq(b) + 2)
                        stats(M.tmp, M.st1, M.mv1, M.var1, S.st1, S.mv1, ph.src_base + b)

            def normalise(G, b, g):
                dve.wait_ge(S.out_ps, NG * seq(b) + g + 1)
                view = G[:, :].rearrange("p (t h e) -> p t h e", t=KT, h=4)
                o, s = view[:, :, :, 0:HD], view[:, :, :, HD]
                att = M.att[:, :, 4 * HD * g:4 * HD * (g + 1)].rearrange("p t (h e) -> p t h e", h=4)
                if g == 0 and (base or not isinstance(b, int) or b > 0):
                    dve.wait_ge(S.attT_ps, 2 * seq(b))
                wide = [P, KT, 4, HD]
                if causal:
                    st = 4 * (NG * b + g)
                    nc.vector.tensor_scalar(M.e8[:, :, :], s, 1e-6, 1e-8, ALU.add, ALU.mult).then_inc(S.norm_step, 1)
                    dve.wait_ge(S.norm_step, st + 1)
                    nc.vector.scalar_tensor_tensor(out=M.den[:, :, :], in0=M.e8[:, :, :], scalar=float(T), in1=s,
                                                   op0=ALU.mult, op1=ALU.add).then_inc(S.norm_step, 1)
                    dve.wait_ge(S.v_all, b + 1)
                    nc.vector.tensor_tensor(M.floor_v[:, :, :, :], M.e8[:, :, :].unsqueeze(3).to_broadcast(wide),
                                            M.v_all[:, 64 * g:64 * g + 64].rearrange("p (h e) -> p h e", h=4).unsqueeze(1).to_broadcast(wide),
                                            ALU.mult)
                    dve.wait_ge(S.norm_step, st + 2)
                    nc.vector.reciprocal(M.rden[:, :, :], M.den[:, :, :]).then_inc(S.norm_step, 1)
                    dve.wait_ge(S.norm_step, st + 3)
                    nc.vector.tensor_tensor(M.floor_v[:, :, :, :], M.floor_v[:, :, :, :], o, ALU.add).then_inc(S.norm_step, 1)
                    dve.wait_ge(S.norm_step, st + 4)
                    nc.vector.tensor_tensor(att, M.floor_v[:, :, :, :], M.rden[:, :, :].unsqueeze(3).to_broadcast(wide),
                                            ALU.mult).then_inc(S.att_ready, 1)
                else:
                    dve.wait_ge(S.att_ready, NG * seq(b) + g)
                    nc.vector.reciprocal(M.rden[:, :, :], s).then_inc(S.rden, 1)
                    dve.wait_ge(S.rden, NG * (ph.src_base + b) + g + 1)
                    nc.vector.tensor_tensor(att, o, M.rden[:, :, :].unsqueeze(3).to_broadcast(wide), ALU.mult).then_inc(S.att_ready, 1)

            def stats(src, st, mv, var, st_sem, mv_sem, n):
                for t in range(KT):
                    last = nc.vector.bn_stats(st[:, t, :], src[:, t, :])
                last.then_inc(st_sem, 1)
                dve.wait_ge(st_sem, n + 1)
                nc.vector.memset(var[:, :], EPS)
                for t in range(KT):
                    last = nc.vector.bn_aggr(mv[:, t, :], st[:, t, :])
                last.then_inc(mv_sem, 1)

            def norm_stats(b):
                if not exists(b):
                    return
                dve.wait_ge(S.x_loaded, 16 * (seq(b) + 1))
                if base or not isinstance(b, int) or b > 0:
                    dve.wait_ge(S.xn_ready, seq(b))
                stats(M.x_in, M.st0, M.mv0, M.var0, S.st0, S.mv0, seq(b))

            def apply_norm(src, mv, rstd, dst, done):
                for t in range(KT):
                    last = nc.vector.tensor_scalar(dst[:, t, :], src[:, t, :], mv[:, t, 0:1], rstd[:, t:t + 1],
                                                   ALU.subtract, ALU.mult)
                last.then_inc(done, 1)

            def norm_x(b):
                if not exists(b):
                    return
                if base or not isinstance(b, int) or b > 0:
                    dve.wait_ge(S.xnT_ps, 2 * seq(b))
                if ph.ffn and (ph.src_base or not isinstance(b, int) or b > 0):
                    dve.wait_ge(S.src_saved, 16 * (ph.src_base + b))
                dve.wait_ge(S.rstd0, seq(b) + 1)
                apply_norm(M.x_in, M.mv0, M.rstd0, M.xn, S.xn_ready)

            def norm_y(b):
                if not (exists(b) and ph.ffn):
                    return
                n = ph.src_base + b
                if ph.src_base or not isinstance(b, int) or b > 0:
                    dve.wait_ge(S.x_stored, 16 * seq(b))
                dve.wait_ge(S.rstd1, n + 1)
                apply_norm(M.tmp, M.mv1, M.rstd1, M.x_out, S.x1_normed)

            def body(b):
                for g in range(NG):
                    sb, sg = group_ahead(b, g, 2)
                    for kt in range(KT):
                        for i in range(4):
                            if exists(sb):
                                row_max(sb, sg, kt, i)
                            if causal:
                                clip(b, g, kt, i)
                        if kt == KT - 1 and exists(sb):
                            split_max(sb, sg)
                        for at, what, n, idx in uses((g, kt), b):
                            read_bank(at, what, n, idx)
                        if (g, kt) == (2, 2):
                            norm_y(b - 1)
                        if (g, kt) == (3, 1):
                            norm_stats(b + 2)
                        if (g, kt) == (3, 3):
                            norm_x(b + 2)

            norm_stats(0)
            norm_x(0)
            norm_stats(1)
            for at, (_, what, off, idx) in enumerate(USES):
                if off == 1 and what == "v":
                    read_bank(at, what, 0, idx)
            norm_x(1)
            for g in (0, 1):
                for i in range(4):
                    for qt in range(KT):
                        row_max(0, g, i, qt)
                if g == 1:
                    read_bank(18, "max", 0, 0)
                split_max(0, g)
            bodies(dve, body)
            for at, (_, what, off, idx) in enumerate(USES):
                if off == -1:
                    read_bank(at, what, NB - 1, idx)
            norm_y(NB - 1)

        @block.gpsimd
        def _(pool):
            def inv_std(mv, var, rstd, mv_sem, var_sem, rstd_sem, n):
                pool.wait_ge(mv_sem, n + 1)
                nc.gpsimd.tensor_tensor(var[:, :], var[:, :], mv[:, :, 1], ALU.add).then_inc(var_sem, 1)
                pool.wait_ge(var_sem, n + 1)
                nc.gpsimd.tensor_tensor(rstd[:, :], var[:, :], C.minus_half[:, :], ALU.pow).then_inc(rstd_sem, 1)

            def inv_std_x(b):
                if exists(b):
                    inv_std(M.mv0, M.var0, M.rstd0, S.mv0, S.var0, S.rstd0, seq(b))

            def inv_std_y(b):
                if exists(b) and ph.ffn:
                    inv_std(M.mv1, M.var1, M.rstd1, S.mv1, S.var1, S.rstd1, ph.src_base + b)

            def split(b, j):
                st = 3 * (4 * seq(b) + j)
                pool.wait_ge(S.qkf_ready, 4 * seq(b) + j + 1)
                full, first = M.qkf[:, j, :], M.parts[:, j, 0, :]
                nc.gpsimd.tensor_tensor(M.parts[:, j, 1, :], full, first, ALU.subtract).then_inc(S.split_step, 1)
                pool.wait_ge(S.split_step, st + 1)
                nc.gpsimd.tensor_tensor(M.rest[:, :], full, first, ALU.subtract).then_inc(S.split_step, 1)
                pool.wait_ge(S.split_step, st + 2)
                nc.gpsimd.tensor_tensor(M.parts[:, j, 2, :], M.rest[:, :], M.parts[:, j, 1, :], ALU.subtract).then_inc(S.split_step, 1)

            def lay_out_v(b, g):
                if g == 0:
                    pool.wait_ge(S.v_sb, 2 * seq(b) + 2)
                if base or not isinstance(b, int) or b > 0:
                    pool.wait_ge(S.pv_done, pv_count(b, g, KT - 1) - NG * KT)
                hs = slice(4 * g, 4 * g + 4)
                last = nc.gpsimd.tensor_tensor(M.v_aug[:, :, hs, 0:HD],
                                               M.v_st[:, :, 64 * g:64 * g + 64].rearrange("p t (h e) -> p t h e", h=4),
                                               C.ones[:, 0:64].rearrange("p (h e) -> p h e", h=4).unsqueeze(1).to_broadcast([P, KT, 4, HD]),
                                               ALU.mult)
                if causal:
                    last.then_inc(S.v_step, 1)
                    st = 2 * (NG * b + g)
                    pool.wait_ge(S.v_step, st + 1)
                    nc.gpsimd.tensor_tensor(M.v_later[:, 1, hs, :], M.v_aug[:, 3, hs, :], M.v_aug[:, 2, hs, :], ALU.add).then_inc(S.v_step, 1)
                    pool.wait_ge(S.v_step, st + 2)
                    last = nc.gpsimd.tensor_tensor(M.v_later[:, 0, hs, :], M.v_later[:, 1, hs, :], M.v_aug[:, 1, hs, :], ALU.add)
                last.then_inc(S.v_aug, 1)

            def sum_v(b):
                if not causal:
                    return
                pool.wait_ge(S.v_sb, 2 * seq(b) + 2)
                if not isinstance(b, int) or b > 0:
                    pool.wait_ge(S.max_ps, NG * seq(b) - 2)
                pairs = M.v_st[:, :, :].rearrange("p (a t) d -> p a t d", a=2)
                nc.gpsimd.tensor_tensor(M.v_pair[:, :, :], pairs[:, :, 0, :], pairs[:, :, 1, :], ALU.add).then_inc(S.v_pair, 1)
                pool.wait_ge(S.v_pair, b + 1)
                nc.gpsimd.tensor_tensor(M.v_tot[:, :], M.v_pair[:, 0, :], M.v_pair[:, 1, :], ALU.add).then_inc(S.v_total, 1)

            def add_bias(b):
                if not (exists(b) and ph.ffn):
                    return
                pool.wait_ge(S.res_loaded, 16 * (seq(b) + 1))
                nc.gpsimd.tensor_tensor(M.res[:, :, :], M.res[:, :, :], ph.b_o[:, :].unsqueeze(1).to_broadcast([P, KT, D]),
                                        ALU.add).then_inc(S.res_biased, 1)

            def scale_y(b):
                if not (exists(b) and ph.ffn):
                    return
                n = ph.src_base + b
                pool.wait_ge(S.x1_normed, n + 1)
                nc.gpsimd.tensor_tensor(M.x_out[:, :, :], M.x_out[:, :, :], C.ln1_g[:, :].unsqueeze(1).to_broadcast([P, KT, D]),
                                        ALU.mult).then_inc(S.x1_scaled, 1)
                pool.wait_ge(S.x1_scaled, n + 1)
                nc.gpsimd.tensor_tensor(M.x_out[:, :, :], M.x_out[:, :, :], C.ln1_b[:, :].unsqueeze(1).to_broadcast([P, KT, D]),
                                        ALU.add).then_inc(S.x1_ready, 1)

            def body(b):
                add_bias(b - 1)
                if exists(b + 1):
                    for j in range(4):
                        split(b + 1, j)
                    lay_out_v(b + 1, 0)
                    sum_v(b + 1)
                inv_std_y(b - 1)
                if exists(b + 1):
                    lay_out_v(b + 1, 1)
                scale_y(b - 1)
                if exists(b + 1):
                    lay_out_v(b + 1, 2)
                inv_std_x(b + 2)
                if exists(b + 1):
                    lay_out_v(b + 1, 3)

            inv_std_x(0)
            inv_std_x(1)
            for j in range(4):
                split(0, j)
            for g in range(NG):
                lay_out_v(0, g)
            sum_v(0)
            bodies(pool, body)
            add_bias(NB - 1)
            inv_std_y(NB - 1)
            scale_y(NB - 1)



def scratch(nc):
    return (nc.dram_tensor("q_parts_d", [NB, H, 3 * HD, T], BF16).ap(),
            nc.dram_tensor("k_parts_d", [NB, H, 6 * HD, T], BF16).ap(),
            nc.dram_tensor("src_d", [NB, T, D], F32).ap())



def attention_memory(nc, ctx, tag, dram):
    def sb(name, shape, dt=F32):
        return ctx.enter_context(nc.sbuf_tensor(f"{name}_{tag}", shape, dt))

    def psum(name):
        return ctx.enter_context(nc.psum_tensor(f"{name}_{tag}", [P, T], F32))

    gen = [psum("gen0"), psum("gen1")]
    M = Names()
    M.q_parts_d, M.k_parts_d, M.src_d = dram
    M.x_in = sb("x_in", [P, KT, D])
    M.xn = sb("xn", [P, KT, D])
    M.res = sb("res", [P, KT, D])
    M.tmp = sb("tmp", [P, KT, D])
    M.x_out = sb("x_out", [P, KT, D])
    M.st0 = sb("st0", [P, KT, 6])
    M.mv0 = sb("mv0", [P, KT, 2])
    M.var0 = sb("var0", [P, KT])
    M.rstd0 = sb("rstd0", [P, KT])
    M.st1 = sb("st1", [P, KT, 6])
    M.mv1 = sb("mv1", [P, KT, 2])
    M.var1 = sb("var1", [P, KT])
    M.rstd1 = sb("rstd1", [P, KT])
    M.xnT = sb("xnT", [P, DC, T])
    M.qkf = sb("qkf", [P, 4, T])
    M.parts = sb("parts", [P, 4, 3, T], BF16)
    M.rest = sb("rest", [P, T])
    M.v_st = sb("v_st", [P, KT, D])
    M.v_aug = sb("v_aug", [P, KT, H, 32])
    M.v_later = sb("v_later", [P, KT - 2, H, 32])
    M.v_pair = sb("v_pair", [P, 2, D])
    M.v_tot = sb("v_tot", [P, D])
    M.v_all = sb("v_all", [P, D])
    M.stack_q = sb("stack_q", [99, NG, 4, T], BF16)
    M.stack_k = sb("stack_k", [99, NG, 4, T], BF16)
    M.neg_max = sb("neg_max", [P, KT, 4])
    M.max_rest = sb("max_rest", [P, KT, 4])
    M.max_parts = sb("max_parts", [P, KT, 3, 4], BF16)
    M.max_sb = sb("max_sb", [12, 2, T], BF16)
    M.prob = sb("prob", [P, 2, 4, T])
    M.floor = sb("floor", [P, 2, 4, T])
    M.o_sb = sb("o_sb", [P, T])
    M.e8 = sb("e8", [P, KT, 4])
    M.den = sb("den", [P, KT, 4])
    M.rden = sb("rden", [P, KT, 4])
    M.floor_v = sb("floor_v", [P, KT, 4, HD])
    M.att = sb("att", [P, KT, D])
    M.attT = sb("attT", [P, DC, T])
    M.sc = [psum("sc0"), psum("sc1")]
    M.sct = [psum("sct0"), psum("sct1")]
    M.out = [psum("out0"), psum("out1")]
    M.gen = gen
    M.gen_bf = [t[:, :].bitcast(BF16) for t in gen]
    return M


def attention_preset(nc, M, S, done):
    with nc.Block() as block:
        @block.vector
        def _(dve):
            nc.vector.memset(M.v_aug[:, :, :, :], 0.0).then_inc(S.preset, 1)
            nc.vector.memset(M.stack_k[96:99, :, :, :], 1.0)
            dve.wait_ge(S.preset, done + 1)
            nc.vector.memset(M.v_aug[:, :, :, HD:HD + 1], 1.0).then_inc(S.preset, 1)


def semaphores(nc, ctx):
    def sem(name):
        return ctx.enter_context(nc.semaphore("s_" + name))

    S = Names()
    S.x_loaded = sem("x_loaded")
    S.xn_ready = sem("xn_ready")
    S.src_saved = sem("src_saved")
    S.res_loaded = sem("res_loaded")
    S.res_biased = sem("res_biased")
    S.x1_normed = sem("x1_normed")
    S.x1_scaled = sem("x1_scaled")
    S.x1_ready = sem("x1_ready")
    S.x_stored = sem("x_stored")
    S.xnT_ps = sem("xnT_ps")
    S.xnT_ready = sem("xnT_ready")
    S.qk_ps = sem("qk_ps")
    S.qkf_ready = sem("qkf_ready")
    S.split_step = sem("split_step")
    S.v_ps = sem("v_ps")
    S.v_sb = sem("v_sb")
    S.v_pair = sem("v_pair")
    S.v_total = sem("v_total")
    S.v_all = sem("v_all")
    S.v_step = sem("v_step")
    S.v_aug = sem("v_aug")
    S.sc_ps = sem("sc_ps")
    S.max_done = sem("max_done")
    S.max_clip = sem("max_clip")
    S.max_split = sem("max_split")
    S.max_ps = sem("max_ps")
    S.max_sb = sem("max_sb")
    S.t_ps = sem("t_ps")
    S.exp_done = sem("exp_done")
    S.clip_done = sem("clip_done")
    S.pv_done = sem("pv_done")
    S.o_sb = sem("o_sb")
    S.out_ps = sem("out_ps")
    S.norm_step = sem("norm_step")
    S.rden = sem("rden")
    S.att_ready = sem("att_ready")
    S.attT_ps = sem("attT_ps")
    S.attT_ready = sem("attT_ready")
    S.y_ps = sem("y_ps")
    S.y_sb = sem("y_sb")
    S.st0 = sem("st0")
    S.mv0 = sem("mv0")
    S.var0 = sem("var0")
    S.rstd0 = sem("rstd0")
    S.st1 = sem("st1")
    S.mv1 = sem("mv1")
    S.var1 = sem("var1")
    S.rstd1 = sem("rstd1")
    S.preset = sem("preset")
    S.made = sem("made")
    S.consts_loaded = sem("consts_loaded")
    S.parts_written = [sem(f"parts_written{i}") for i in range(2)]
    S.stack_loaded = [sem(f"stack_loaded{i}") for i in range(NG)]
    S.max_rows = [sem(f"max_rows{i}") for i in range(NG)]
    return S


def constants(nc, ctx, S, A):
    def sb(name, shape, dt=F32):
        return ctx.enter_context(nc.sbuf_tensor(name, shape, dt))

    C = Names()
    C.ident = sb("ident", [P, P])
    C.ident_bf = sb("ident_bf", [P, P], BF16)
    C.ones = sb("ones", [P, P])
    C.mask_qk = sb("mask_qk", [P, P], BF16)
    C.mask_kq = sb("mask_kq", [P, P], BF16)
    C.minus100 = sb("minus100", [P, 1])
    C.minus_half = sb("minus_half", [P, KT])
    C.no_bias = sb("no_bias", [P, 4])
    C.b_qk = sb("b_qk", [P, 4])
    C.b_v = sb("b_v", [P, D])
    C.b_o = sb("b_o", [P, D])
    C.ln1_g = sb("ln1_g", [P, D])
    C.ln1_b = sb("ln1_b", [P, D])
    C.wa_qkv = sb("wa_qkv", [P, DC, 3 * D])
    C.wa_o = sb("wa_o", [P, DC, D])
    C.wf_qkv = sb("wf_qkv", [P, DC, 3 * D])
    C.wf_o = sb("wf_o", [P, DC, D])

    def row(ap):
        return ap.unsqueeze(0).to_broadcast([P, D])

    with nc.Block() as block:
        @block.sync
        def _(sp):
            n = 0
            for dst, src in ((C.wa_qkv[:, :, :], A["a_w_qkv"].rearrange("(c p) o -> p c o", p=P)),
                             (C.wa_o[:, :, :], A["a_w_proj"].rearrange("(c p) o -> p c o", p=P)),
                             (C.wf_qkv[:, :, 0:D], A["f_Wq"].rearrange("(c p) o -> p c o", p=P)),
                             (C.wf_qkv[:, :, D:2 * D], A["f_Wk"].rearrange("(c p) o -> p c o", p=P)),
                             (C.wf_qkv[:, :, 2 * D:3 * D], A["f_Wv"].rearrange("(c p) o -> p c o", p=P)),
                             (C.wf_o[:, :, :], A["f_Wo"].rearrange("(c p) o -> p c o", p=P)),
                             (C.b_v[:, :], row(A["f_bv"])), (C.b_o[:, :], row(A["f_bo"])),
                             (C.ln1_g[:, :], row(A["f_ln1_g"])), (C.ln1_b[:, :], row(A["f_ln1_b"]))):
                sp.dma_start(dst, src).then_inc(S.consts_loaded, 16)
                n += 16
            for half in range(2):
                for isk, b in enumerate((A["f_bq"], A["f_bk"])):
                    j = 2 * half + isk
                    sp.dma_start(C.b_qk[:, j:j + 1], b[P * half:P * half + P].unsqueeze(1)).then_inc(S.consts_loaded, 16)
                    n += 16
            sp.wait_ge(S.consts_loaded, n)

        @block.gpsimd
        def _(pool):
            pool.memset(C.ident[:, :], 0.0)
            pool.memset(C.ident_bf[:, :], 0.0)
            pool.memset(C.mask_qk[:, :], 0.0)
            pool.memset(C.mask_kq[:, :], 0.0)
            pool.memset(C.ones[:, :], 1.0)
            pool.memset(C.minus100[:, :], -100.0)
            pool.memset(C.no_bias[:, :], 0.0)
            pool.memset(C.minus_half[:, :], -0.5).then_inc(S.made, 1)
            pool.wait_ge(S.made, 1)
            pool.affine_select(out=C.ident[:, :], in_=C.ident[:, :], compare_op=ALU.not_equal, fill=1.0, base=0,
                               pattern=[[-1, P]], channel_multiplier=1)
            pool.affine_select(out=C.ident_bf[:, :], in_=C.ident_bf[:, :], compare_op=ALU.not_equal, fill=1.0, base=0,
                               pattern=[[-1, P]], channel_multiplier=1)
            pool.affine_select(out=C.mask_qk[:, :], in_=C.mask_qk[:, :], compare_op=ALU.is_ge, fill=MASKED, base=0,
                               pattern=[[-1, P]], channel_multiplier=1)
            pool.affine_select(out=C.mask_kq[:, :], in_=C.mask_kq[:, :], compare_op=ALU.is_ge, fill=MASKED, base=0,
                               pattern=[[1, P]], channel_multiplier=-1).then_inc(S.made, 1)
    with nc.Block() as block:
        @block.vector
        def _(dve):
            for half in range(2):
                nc.vector.tensor_scalar(C.b_qk[:, 2 * half:2 * half + 1], C.b_qk[:, 2 * half:2 * half + 1], SCALE, None, ALU.mult)
    return C



SLOTS = NT + NE - 1


def experts(nc, sems, ctx, C, A, k, x_src, x1_d, x_dst):
    s0, b0 = SLOTS * k, NB * k
    def sb(name, shape, dt=F32):
        return ctx.enter_context(nc.sbuf_tensor(f"{name}_e{k}", shape, dt))

    def psum(name):
        return ctx.enter_context(nc.psum_tensor(f"{name}_ps_e{k}", [P, T], F32))

    def sem(name):
        if name not in sems:
            sems[name] = nc.alloc_semaphore(name=f"s_{name}_e")
        return sems[name]

    sorted_x = nc.dram_tensor(f"sorted_x_{k}", [SLOTS * P, D], F32).ap()
    sorted_y = nc.dram_tensor(f"sorted_y_{k}", [SLOTS * P, D], F32).ap()

    w1, w2 = sb("w1", [P, DC, NE, F]), sb("w2", [P, FC, NE, D])
    b1, b2 = sb("b1", [P, NE, F]), sb("b2", [P, NE, D])
    g2, be2, rw, rb = sb("g2", [P, D]), sb("be2", [P, D]), sb("rw", [P, D]), sb("rb", [P, 1])
    x1 = sb("x1", [P, NT, D])
    zero = sb("zero", [P, 5, D])
    tri = sb("tri", [P, P])
    prod = sb("prod", [P, KT, D])
    keys, adj, choice = sb("keys", [P, NT]), sb("adj", [P, NT]), sb("choice", [P, NT])
    key_i, pos_i = sb("key_i", [P, NT], I32), sb("pos_i", [P, NT], I32)
    onehot, total, pos3 = sb("onehot", [P, NE, NT]), sb("total", [P, NE, NT]), sb("pos3", [P, NE, NT])
    scan = [sb("scan0", [P, NE, NT]), sb("scan1", [P, NE, NT])]
    pos = sb("pos", [P, NT])
    tiles_i, tiles, first_tile, first_row = sb("tiles_i", [P, NE], I32), sb("tiles", [P, NE]), sb("first_tile", [P, NE]), sb("first_row", [P, NE])
    slot_no, slot_e, slot_ge = sb("slot_no", [P, SLOTS]), sb("slot_e", [P, SLOTS]), sb("slot_ge", [P, SLOTS])
    slot_no_i, slot_e_i = sb("slot_no_i", [P, SLOTS], I32), sb("slot_e_i", [P, SLOTS], I32)
    xt, xT, h, hT, y = sb("xt", [P, D]), sb("xT", [P, DC, P]), sb("h", [P, F]), sb("hT", [P, FC, P]), sb("y", [P, D])
    got, x_prev, out = ([sb(f"{n}{i}", [P, KT, D]) for i in range(2)] for n in ("got", "x_prev", "out"))
    st, mv = [sb(f"st{i}", [P, KT, 6]) for i in range(2)], [sb(f"mv{i}", [P, KT, 2]) for i in range(2)]
    var, rstd = [sb(f"var{i}", [P, KT]) for i in range(2)], [sb(f"rstd{i}", [P, KT]) for i in range(2)]

    rank_ps, xT_ps, y_ps = psum("rank"), psum("xT"), psum("y")
    h_ps, hT_ps = [psum("h0"), psum("h1")], [psum("hT0"), psum("hT1")]

    x1_loaded = [sem(f"x1_loaded{b}") for b in range(NB)]
    params, weights, prod_done, keys_done, step = sem("params"), sem("weights"), sem("prod_done"), sem("keys_done"), sem("step")
    made, onehot_ready, ranked, routed = sem("made"), sem("onehot_ready"), sem("ranked"), sem("routed")
    zeroed, scattered = sem("zeroed"), sem("scattered")
    xt_loaded, xT_made, xT_ready, h_made, h_ready = sem("xt_loaded"), sem("xT_made"), sem("xT_ready"), sem("h_made"), sem("h_ready")
    hT_made, hT_ready, y_made, y_ready, y_stored = sem("hT_made"), sem("hT_ready"), sem("y_made"), sem("y_ready"), sem("y_stored")
    gathered, prev_loaded, stored = ([sem(f"{n}{i}") for i in range(2)] for n in ("gathered", "prev_loaded", "stored"))
    summed, st_done, mv_done, var_done, rstd_done = sem("summed"), sem("st_done"), sem("mv_done"), sem("var_done"), sem("rstd_done")
    normed, scaled, shifted, finished = sem("normed"), sem("scaled"), sem("shifted"), sem("finished")

    def slots(eng, tile):
        tile(0, True, False)
        with eng.Fori(1, SLOTS - 1, 1) as s:
            tile(s, False, False)
        tile(SLOTS - 1, False, True)

    def pairs(eng, one):
        for i in range(2):
            one(i, i)
        with eng.Fori(1, NB // 2, 1) as pair:
            for i in range(2):
                one(2 * pair + i, i)

    def later(b):
        return not isinstance(b, int) or b >= 2

    with nc.Block() as block:

        @block.sync
        def _(sp):
            for b in range(NB):
                sp.dma_start(x1[:, KT * b:KT * b + KT, :], x1_d[b].rearrange("(t p) d -> p t d", p=P)).then_inc(x1_loaded[b], 16)
                if b == 0:
                    sp.dma_start(rw[:, :], A["f_router_w"].rearrange("d o -> o d").to_broadcast([P, D])).then_inc(params, 16)
                    sp.dma_start(rb[:, :], A["f_router_b"].unsqueeze(0).to_broadcast([P, 1])).then_inc(params, 16)
            sp.wait_ge(made, 3 * k + 1)
            for s in range(0, SLOTS, 5):
                sp.dma_start(sorted_x[s * P:(s + 5) * P, :].rearrange("(t p) d -> p t d", p=P), zero[:, :, :]).then_inc(zeroed, 16)
            for e in range(NE):
                sp.dma_start(w1[:, :, e, :], A["f_W1"][e].rearrange("(c p) f -> p c f", p=P)).then_inc(weights, 16)
                sp.dma_start(w2[:, :, e, :], A["f_W2"][e].rearrange("(c p) d -> p c d", p=P)).then_inc(weights, 16)
                sp.dma_start(b1[:, e, :], A["f_b1"][e:e + 1, :].to_broadcast([P, F])).then_inc(weights, 16)
                sp.dma_start(b2[:, e, :], A["f_b2"][e:e + 1, :].to_broadcast([P, D])).then_inc(weights, 16)
            sp.dma_start(g2[:, :], A["f_ln2_g"].unsqueeze(0).to_broadcast([P, D])).then_inc(weights, 16)
            sp.dma_start(be2[:, :], A["f_ln2_b"].unsqueeze(0).to_broadcast([P, D])).then_inc(weights, 16)

            def load_prev(b, i):
                if later(b):
                    sp.wait_ge(finished, b0 + b - 1)
                sp.dma_start(x_prev[i][:, :, :], x_src[b].rearrange("(t p) d -> p t d", p=P)).then_inc(prev_loaded[i], 16)

            def store(b, i):
                sp.wait_ge(finished, b0 + b + 1)
                sp.dma_start(x_dst[b].rearrange("(t p) d -> p t d", p=P), out[i][:, :, :]).then_inc(stored[i], 16)

            load_prev(0, 0)
            load_prev(1, 1)
            for i in range(2):
                store(i, i)
            with sp.Fori(1, NB // 2, 1) as pair:
                for i in range(2):
                    load_prev(2 * pair + i, i)
                for i in range(2):
                    store(2 * pair + i, i)
            for i in range(2):
                sp.wait_ge(stored[i], 16 * (NB // 2) * (k + 1))

        @block.tensor
        def _(pe):
            pe.wait_ge(made, 3 * k + 3)
            pe.wait_ge(onehot_ready, k + 1)
            oh = onehot[:, :, :].rearrange("p e t -> p (e t)")
            nc.tensor.matmul(rank_ps[:, 0:P], tri[:, :], oh, start=True, stop=True)
            nc.tensor.matmul(rank_ps[:, P:2 * P], C.ones[:, :], oh, start=True, stop=True).then_inc(ranked, 1)

            def expert_of(s):
                return pe.value_load(slot_e_i[0:1, bass.ds(s, 1)], min_val=0, max_val=NE - 1)

            def transpose_x(s):
                pe.wait_ge(xt_loaded, 16 * ((s0 + s) + 1))
                if not (isinstance(s, int) and s == 0):
                    pe.wait_ge(xT_ready, s0 + s)
                for c in range(DC):
                    last = nc.tensor.transpose(xT_ps[:, c * P:c * P + P], xt[:, c * P:c * P + P], C.ident[:, :])
                last.then_inc(xT_made, 1)

            def second(s):
                e = expert_of(s)
                pe.wait_ge(hT_ready, 2 * (s0 + s) + 2)
                if not (isinstance(s, int) and s == 0):
                    pe.wait_ge(y_ready, s0 + s)
                for c in range(FC):
                    last = nc.tensor.matmul(y_ps[:, 0:D], hT[:, c, :], w2[:, c, e, :], start=(c == 0), stop=(c == FC - 1))
                last.then_inc(y_made, 1)

            def tile(s, first, last_one):
                e = expert_of(s)
                pe.wait_ge(xT_ready, s0 + s + 1)
                for f in range(2):
                    if not first:
                        pe.wait_ge(h_ready, 2 * (s0 + s) - 1 + f)
                    for c in range(DC):
                        last = nc.tensor.matmul(h_ps[f][:, :], xT[:, c, :], w1[:, c, e, T * f:T * f + T], start=(c == 0), stop=(c == DC - 1))
                    last.then_inc(h_made, 1)
                if not last_one:
                    transpose_x(s + 1)
                if not first:
                    second(s - 1)
                for f in range(2):
                    pe.wait_ge(h_ready, 2 * (s0 + s) + f + 1)
                    if not first:
                        pe.wait_ge(hT_ready, 2 * (s0 + s) - 1 + f)
                    for c in range(4):
                        last = nc.tensor.transpose(hT_ps[f][:, c * P:c * P + P], h[:, T * f + c * P:T * f + c * P + P], C.ident[:, :])
                    last.then_inc(hT_made, 1)

            transpose_x(0)
            pe.wait_ge(weights, 16 * (4 * NE + 2) * (k + 1))
            pe.wait_ge(routed, k + 1)
            slots(pe, tile)
            second(SLOTS - 1)

        @block.scalar
        def _(act):
            def load(s):
                act.dma_start(xt[:, :], sorted_x.rearrange("(s p) d -> s p d", p=P)[s]).then_inc(xt_loaded, 16)

            def read_xT(s, first):
                act.wait_ge(xT_made, s0 + s + 1)
                if not first:
                    act.wait_ge(h_made, 2 * (s0 + s))
                nc.scalar.activation(xT[:, :, :], xT_ps[:, 0:D].rearrange("p (c t) -> p c t", c=DC), ACT.Copy).then_inc(xT_ready, 1)

            def tile(s, first, last_one, load_more=True):
                if not last_one:
                    read_xT(s + 1, False)
                    if load_more:
                        load(s + 2)
                for f in range(2):
                    act.wait_ge(hT_made, 2 * (s0 + s) + f + 1)
                    if not first and f == 0:
                        act.wait_ge(y_made, s0 + s)
                    nc.scalar.activation(hT[:, 4 * f:4 * f + 4, :], hT_ps[f][:, :].rearrange("p (c t) -> p c t", c=4), ACT.Relu).then_inc(hT_ready, 1)

            act.wait_ge(scattered, 16 * NT * (k + 1))
            act.wait_ge(zeroed, 16 * (SLOTS // 5) * (k + 1))
            load(0)
            read_xT(0, True)
            load(1)
            tile(0, True, False)
            with act.Fori(1, SLOTS - 2, 1) as s:
                tile(s, False, False)
            tile(SLOTS - 2, False, False, load_more=False)
            tile(SLOTS - 1, False, True)

        @block.vector
        def _(dve):
            dve.wait_ge(params, 32 * (k + 1))
            for b in range(NB):
                dve.wait_ge(x1_loaded[b], 16 * (k + 1))
                if b >= 1:
                    dve.wait_ge(keys_done, b0 + b)
                nc.vector.tensor_tensor(prod[:, :, :], x1[:, KT * b:KT * b + KT, :], rw[:, :].unsqueeze(1).to_broadcast([P, KT, D]),
                                        ALU.mult).then_inc(prod_done, 1)
                dve.wait_ge(prod_done, b0 + b + 1)
                nc.vector.tensor_reduce(keys[:, KT * b:KT * b + KT], prod[:, :, :], AX.X, ALU.add).then_inc(keys_done, 1)
            dve.wait_ge(keys_done, b0 + NB)

            steps = sems.setdefault("links", [0])

            def link(ins):
                steps[0] += 1
                ins.then_inc(step, 1)
                dve.wait_ge(step, steps[0])

            link(nc.vector.tensor_scalar(keys[:, :], keys[:, :], rb[:, 0:1], None, ALU.add))
            link(nc.vector.tensor_copy(key_i[:, :], keys[:, :]))
            link(nc.vector.tensor_copy(choice[:, :], key_i[:, :]))
            link(nc.vector.tensor_tensor(adj[:, :], choice[:, :], keys[:, :], ALU.is_gt))
            link(nc.vector.tensor_tensor(choice[:, :], choice[:, :], adj[:, :], ALU.subtract))
            link(nc.vector.tensor_copy(key_i[:, :], choice[:, :]))
            link(nc.vector.tensor_scalar(key_i[:, :], key_i[:, :], NE - 1, None, ALU.bitwise_and))
            link(nc.vector.tensor_copy(choice[:, :], key_i[:, :]))
            for e in range(NE):
                last = nc.vector.tensor_scalar(onehot[:, e, :], choice[:, :], float(e), None, ALU.is_equal)
            last.then_inc(onehot_ready, 1)
            dve.wait_ge(onehot_ready, k + 1)
            dve.wait_ge(ranked, k + 1)
            ranks = rank_ps[:, 0:2 * P].rearrange("p (a e t) -> p a e t", a=2, e=NE)
            nc.vector.tensor_copy(total[:, :, :], ranks[:, 1, :, :])
            link(nc.vector.tensor_copy(scan[0][:, :, :], ranks[:, 1, :, :]))
            a, b = scan
            hop = 1
            while hop < NT:
                nc.vector.tensor_copy(b[:, :, 0:hop], a[:, :, 0:hop])
                link(nc.vector.tensor_tensor(b[:, :, hop:NT], a[:, :, hop:NT], a[:, :, 0:NT - hop], ALU.add))
                a, b = b, a
                hop *= 2
            link(nc.vector.tensor_scalar(tiles_i[:, :], a[:, :, NT - 1], float(P - 1), None, ALU.add))
            link(nc.vector.tensor_scalar(tiles_i[:, :], tiles_i[:, :], P.bit_length() - 1, None, ALU.logical_shift_right))
            nc.vector.memset(first_tile[:, 0:1], 0.0)
            link(nc.vector.tensor_copy(tiles[:, :], tiles_i[:, :]))
            for e in range(1, NE):
                link(nc.vector.tensor_tensor(first_tile[:, e:e + 1], first_tile[:, e - 1:e], tiles[:, e - 1:e], ALU.add))
            link(nc.vector.tensor_scalar(first_row[:, :], first_tile[:, :], float(P), None, ALU.mult))
            link(nc.vector.tensor_tensor(pos3[:, :, :], a[:, :, :], total[:, :, :], ALU.subtract))
            link(nc.vector.tensor_tensor(pos3[:, :, :], ranks[:, 0, :, :], pos3[:, :, :], ALU.add))
            link(nc.vector.tensor_tensor(pos3[:, :, :], pos3[:, :, :], first_row[:, :].unsqueeze(2).to_broadcast([P, NE, NT]), ALU.add))
            link(nc.vector.tensor_tensor(pos3[:, :, :], pos3[:, :, :], onehot[:, :, :], ALU.mult))
            link(nc.vector.tensor_reduce(pos[:, :], pos3[:, :, :].rearrange("p e t -> p t e"), AX.X, ALU.add))
            nc.vector.tensor_copy(pos_i[:, :], pos[:, :])
            dve.wait_ge(made, 3 * k + 2)
            link(nc.vector.tensor_copy(slot_no[:, :], slot_no_i[:, :]))
            link(nc.vector.tensor_scalar(slot_e[:, :], slot_no[:, :], first_tile[:, 1:2], None, ALU.is_ge))
            for e in range(2, NE):
                link(nc.vector.tensor_scalar(slot_ge[:, :], slot_no[:, :], first_tile[:, e:e + 1], None, ALU.is_ge))
                link(nc.vector.tensor_tensor(slot_e[:, :], slot_e[:, :], slot_ge[:, :], ALU.add))
            nc.vector.tensor_copy(slot_e_i[:, :], slot_e[:, :]).then_inc(routed, 1)
            dve.wait_ge(routed, k + 1)
            dve.wait_ge(weights, 16 * (4 * NE + 2) * (k + 1))

            def expert_of(s):
                return dve.value_load(slot_e_i[0:1, bass.ds(s, 1)], min_val=0, max_val=NE - 1)

            def add_b2(s, first):
                e = expert_of(s)
                dve.wait_ge(y_made, s0 + s + 1)
                if not first:
                    dve.wait_ge(y_stored, 16 * (s0 + s))
                nc.vector.tensor_tensor(y[:, :], y_ps[:, 0:D], b2[:, e, :], ALU.add).then_inc(y_ready, 1)

            def tile(s, first, last_one, second=False):
                e = expert_of(s)
                for f in range(2):
                    dve.wait_ge(h_made, 2 * (s0 + s) + f + 1)
                    if not first:
                        dve.wait_ge(hT_made, 2 * (s0 + s) - 1 + f)
                    nc.vector.tensor_tensor(h[:, T * f:T * f + T], h_ps[f][:, :], b1[:, e, T * f:T * f + T], ALU.add).then_inc(h_ready, 1)
                if not first:
                    add_b2(s - 1, second)

            tile(0, True, False)
            tile(1, False, False, second=True)
            with dve.Fori(2, SLOTS, 1) as s:
                tile(s, False, False)
            add_b2(SLOTS - 1, False)

            def finish(b, i):
                n = (b // 2 + 1) if isinstance(b, int) else None
                turn = (n if n is not None else (b - i) // 2 + 1) + NB // 2 * k
                dve.wait_ge(gathered[i], 16 * KT * turn)
                x = x1[:, bass.ds(KT * b, KT), :] if n is None else x1[:, KT * b:KT * b + KT, :]
                nc.vector.tensor_tensor(got[i][:, :, :], got[i][:, :, :], x, ALU.add).then_inc(summed, 1)
                dve.wait_ge(summed, b0 + b + 1)
                for t in range(KT):
                    last = nc.vector.bn_stats(st[i][:, t, :], got[i][:, t, :])
                last.then_inc(st_done, 1)
                dve.wait_ge(st_done, b0 + b + 1)
                nc.vector.memset(var[i][:, :], EPS)
                for t in range(KT):
                    last = nc.vector.bn_aggr(mv[i][:, t, :], st[i][:, t, :])
                last.then_inc(mv_done, 1)
                dve.wait_ge(rstd_done, b0 + b + 1)
                if later(b):
                    dve.wait_ge(stored[i], 16 * (turn - 1))
                for t in range(KT):
                    last = nc.vector.tensor_scalar(out[i][:, t, :], got[i][:, t, :], mv[i][:, t, 0:1], rstd[i][:, t:t + 1],
                                                   ALU.subtract, ALU.mult)
                last.then_inc(normed, 1)
                dve.wait_ge(normed, b0 + b + 1)
                wide = [P, KT, D]
                nc.vector.tensor_tensor(out[i][:, :, :], out[i][:, :, :], g2[:, :].unsqueeze(1).to_broadcast(wide), ALU.mult).then_inc(scaled, 1)
                dve.wait_ge(scaled, b0 + b + 1)
                nc.vector.tensor_tensor(out[i][:, :, :], out[i][:, :, :], be2[:, :].unsqueeze(1).to_broadcast(wide), ALU.add).then_inc(shifted, 1)
                dve.wait_ge(shifted, b0 + b + 1)
                dve.wait_ge(prev_loaded[i], 16 * turn)
                nc.vector.tensor_tensor(out[i][:, :, :], out[i][:, :, :], x_prev[i][:, :, :], ALU.add).then_inc(finished, 1)

            pairs(dve, finish)

        @block.gpsimd
        def _(pool):
            pool.memset(tri[:, :], 1.0)
            pool.memset(zero[:, :, :], 0.0).then_inc(made, 1)
            pool.iota(slot_no_i[:, :], pattern=[[1, SLOTS]], base=0, channel_multiplier=0).then_inc(made, 1)
            pool.wait_ge(made, 3 * k + 2)
            pool.affine_select(out=tri[:, :], in_=tri[:, :], compare_op=ALU.is_gt, fill=0.0, base=0,
                               pattern=[[1, P]], channel_multiplier=-1).then_inc(made, 1)
            pool.wait_ge(routed, k + 1)
            pool.wait_ge(zeroed, 16 * (SLOTS // 5) * (k + 1))
            for b in range(NB):
                pool.wait_ge(x1_loaded[b], 16 * (k + 1))
                for t in range(KT * b, KT * b + KT):
                    pool.indirect_dma_start(sorted_x, bass.IndirectOffsetOnAxis(ap=pos_i[:, t:t + 1], axis=0),
                                            x1[:, t, :], None).then_inc(scattered, 16)
            with pool.Fori(0, SLOTS, 1) as s:
                pool.wait_ge(y_ready, s0 + s + 1)
                pool.dma_start(sorted_y.rearrange("(s p) d -> s p d", p=P)[s], y[:, :]).then_inc(y_stored, 16)
            pool.wait_ge(y_stored, 16 * (s0 + SLOTS))

            def gather(b, i):
                if later(b):
                    pool.wait_ge(normed, b0 + b - 1)
                for t in range(KT):
                    at = pos_i[:, KT * b + t:KT * b + t + 1] if isinstance(b, int) else pos_i[:, bass.ds(KT * b + t, 1)]
                    pool.indirect_dma_start(got[i][:, t, :], None, sorted_y,
                                            bass.IndirectOffsetOnAxis(ap=at, axis=0)).then_inc(gathered[i], 16)

            def inv_std(b, i):
                pool.wait_ge(mv_done, b0 + b + 1)
                nc.gpsimd.tensor_tensor(var[i][:, :], var[i][:, :], mv[i][:, :, 1], ALU.add).then_inc(var_done, 1)
                pool.wait_ge(var_done, b0 + b + 1)
                nc.gpsimd.tensor_tensor(rstd[i][:, :], var[i][:, :], C.minus_half[:, :], ALU.pow).then_inc(rstd_done, 1)

            for b in range(NB):
                gather(b, b % 2)
                if b >= 1:
                    inv_std(b - 1, (b - 1) % 2)
            inv_std(NB - 1, (NB - 1) % 2)



NTM = NB
NBT = T // P
NREL = 2 * NTM - 1
REL0 = 16 - (NTM - 1)
RING = 3
ON_DVE = (3, 7, 11)


def local_attention(nc, ctx, C, A, x_src, x_dst):
    def sb(name, shape, dt=F32):
        return ctx.enter_context(nc.sbuf_tensor(f"{name}_l", shape, dt))

    def psum(name):
        return ctx.enter_context(nc.psum_tensor(f"{name}_ps_l", [P, T], F32))

    def sem(name):
        return ctx.enter_context(nc.semaphore(f"s_{name}_l"))

    w, w_o, w_nat = sb("w", [P, DC, 3 * D]), sb("w_o", [P, DC, D]), sb("w_nat", [P, DC, D])
    bias, bias_o, bq = sb("bias", [P, 3 * D]), sb("bias_o", [P, D]), sb("bq", [P, DC])
    rel, head, bq_wide = sb("rel", [P, NREL]), sb("head", [P, DC, H]), sb("bq_wide", [P, DC, P])
    rel_heads, w_rel, b_rel = sb("rel_heads", [P, DC, NREL, H]), sb("w_rel", [P, DC, NREL * H]), sb("b_rel", [P, NREL * H])
    x = [sb(f"x{i}", [P, NTM, D]) for i in range(3)]
    st, mv, var, rstd, half = sb("st", [P, NTM, 6]), sb("mv", [P, NTM, 2]), sb("var", [P, NTM]), sb("rstd", [P, NTM]), sb("half", [P, NTM])
    xn, xnT = sb("xn", [P, NTM, D]), sb("xnT", [P, DC, NTM * P])
    qkv = [sb(f"qkv{i}", [P, NTM, 3 * D]) for i in range(2)]
    q_rel = [sb(f"q_rel{i}", [P, NTM, NTM * H]) for i in range(2)]
    prod = [sb(f"prod{i}", [P, NTM * D]) for i in range(RING)]
    score, weight = sb("score", [P, NTM, NTM, H]), sb("weight", [P, NTM, NTM, H])
    peak, total, inv = sb("peak", [P, NTM, H]), sb("total", [P, NTM, H]), sb("inv", [P, NTM, H])
    att, attT, out = sb("att", [P, NTM, D]), sb("attT", [P, DC, 4 * P]), sb("out", [P, NTM, D])
    tr_ps, a_ps, b_ps = ([psum(f"{n}{i}") for i in range(2)] for n in ("tr", "a", "b"))
    oT_ps, y_ps = psum("oT"), psum("y")

    params, made, rel_made, rel_ps, rel_ready = sem("params"), sem("made"), sem("rel_made"), sem("rel_ps"), sem("rel_ready")
    x_loaded = [sem(f"x_loaded{i}") for i in range(3)]
    st_done, mv_done, var_done, rstd_done, xn_ready, x_biased = sem("st_done"), sem("mv_done"), sem("var_done"), sem("rstd_done"), sem("xn_ready"), sem("x_biased")
    tr_made, xnT_ready, a_made, a_ready, b_made, b_ready = sem("tr_made"), sem("xnT_ready"), sem("a_made"), sem("a_ready"), sem("b_made"), sem("b_ready")
    pool_prod, dve_prod, summed = sem("pool_prod"), sem("dve_prod"), sem("summed")
    soft, inv_step, shifted, weights_ready, normed = sem("soft"), sem("inv_step"), sem("shifted"), sem("weights_ready"), sem("normed")
    oT_made, attT_ready, y_made, y_ready, stored = sem("oT_made"), sem("attT_ready"), sem("y_made"), sem("y_ready"), sem("stored")

    x_in = x_src.rearrange("t (n p) d -> n p t d", p=P)
    x_out = x_dst.rearrange("t (n p) d -> n p t d", p=P)
    NPARAM = 16 * (5 + DC + 8)
    n_dve = len(ON_DVE)
    on_pool = [n for n in range(2 * NTM) if n not in ON_DVE]

    def product(eng, bt, n):
        t = n % NTM
        i = bt % 2
        wide = [P, NTM, H, HD]
        dst = prod[(2 * NTM * bt + n) % RING][:, :].rearrange("p (s h e) -> p s h e", s=NTM, h=H)
        if n < NTM:
            a = qkv[i][:, :, D:2 * D].rearrange("p s (h e) -> p s h e", h=H)
            b = qkv[i][:, t, 0:D].rearrange("p (h e) -> p h e", h=H).unsqueeze(1).to_broadcast(wide)
        else:
            a = qkv[i][:, :, 2 * D:3 * D].rearrange("p s (h e) -> p s h e", h=H)
            b = weight[:, t, :, :].unsqueeze(3).to_broadcast(wide)
        return eng.tensor_tensor(dst, a, b, ALU.mult)

    with nc.Block() as block:

        @block.sync
        def _(sp):
            def load(bt):
                if bt >= 3:
                    sp.wait_ge(y_ready, 4 * (bt - 2))
                sp.dma_start(x[bt % 3][:, :, :], x_in[bt]).then_inc(x_loaded[bt % 3], 16)

            load(0)
            sp.dma_start(w_nat[:, :, :], A["b_w_nat"][0:D, :].rearrange("(c p) o -> p c o", p=P)).then_inc(params, 16)
            for g in range(8):
                sp.dma_start(rel[HD * g:HD * g + HD, :], A["b_rel"][0:HD, REL0:REL0 + NREL]).then_inc(params, 16)
            for c in range(DC):
                sp.dma_start(bq[:, c:c + 1], A["b_b_in"][P * c:P * c + P].unsqueeze(1)).then_inc(params, 16)
            sp.dma_start(w[:, :, :], A["b_w_in"].rearrange("(c p) o -> p c o", p=P)).then_inc(params, 16)
            sp.dma_start(w_o[:, :, :], A["b_w_out"].rearrange("(c p) o -> p c o", p=P)).then_inc(params, 16)
            sp.dma_start(bias[:, :], A["b_b_in"].unsqueeze(0).to_broadcast([P, 3 * D])).then_inc(params, 16)
            sp.dma_start(bias_o[:, :], A["b_b_out"].unsqueeze(0).to_broadcast([P, D])).then_inc(params, 16)
            load(1)
            load(2)
            for bt in range(NBT):
                if bt >= 1 and bt + 2 < NBT:
                    load(bt + 2)
                sp.wait_ge(y_ready, 4 * (bt + 1))
                sp.dma_start(x_out[bt], out[:, :, :]).then_inc(stored, 16)
            sp.wait_ge(stored, 16 * NBT)

        @block.tensor
        def _(pe):
            pe.wait_ge(params, NPARAM)
            pe.wait_ge(rel_made, 3)
            for c in range(DC):
                for o in range(DC):
                    nc.tensor.matmul(a_ps[c][:, 0:NREL * H], w_nat[:, o, c * P:c * P + P], rel_heads[:, o, :, :].rearrange("p r h -> p (r h)"),
                                     start=(o == 0), stop=(o == DC - 1))
            for o in range(DC):
                last = nc.tensor.matmul(b_ps[0][:, 0:NREL * H], bq_wide[:, o, :], rel_heads[:, o, :, :].rearrange("p r h -> p (r h)"),
                                        start=(o == 0), stop=(o == DC - 1))
            last.then_inc(rel_ps, 1)

            def project(bt):
                pe.wait_ge(xn_ready, bt + 1)
                for n in range(4):
                    c, q = n % 2, n // 2
                    if 4 * bt + n >= 2:
                        pe.wait_ge(xnT_ready, 4 * bt + n - 1)
                    for t in range(4):
                        last = nc.tensor.transpose(tr_ps[n % 2][:, t * P:t * P + P], xn[:, 4 * q + t, c * P:c * P + P], C.ident[:, :])
                    last.then_inc(tr_made, 1)
                for t in range(NTM):
                    n = NTM * bt + t
                    pe.wait_ge(xnT_ready, 4 * bt + (2 if t < 4 else 4))
                    pe.wait_ge(rel_ready, 1)
                    if n >= 2:
                        pe.wait_ge(a_ready, n - 1)
                    for c in range(DC):
                        last = nc.tensor.matmul(a_ps[t % 2][:, :], xnT[:, c, t * P:t * P + P], w[:, c, 0:2 * D], start=(c == 0), stop=(c == DC - 1))
                    last.then_inc(a_made, 1)
                    if n >= 2:
                        pe.wait_ge(b_ready, n - 1)
                    r0 = (NTM - 1 - t) * H
                    for c in range(DC):
                        nc.tensor.matmul(b_ps[t % 2][:, 0:D], xnT[:, c, t * P:t * P + P], w[:, c, 2 * D:3 * D], start=(c == 0), stop=(c == DC - 1))
                    for c in range(DC):
                        last = nc.tensor.matmul(b_ps[t % 2][:, D:D + P], xnT[:, c, t * P:t * P + P], w_rel[:, c, r0:r0 + P], start=(c == 0), stop=(c == DC - 1))
                    last.then_inc(b_made, 1)

            def finish(bt):
                for q in range(2):
                    for c in range(DC):
                        n = 4 * bt + 2 * q + c
                        pe.wait_ge(normed, 2 * bt + q + 1)
                        if n >= 1:
                            pe.wait_ge(attT_ready, n)
                        for t in range(4):
                            last = nc.tensor.transpose(oT_ps[:, t * P:t * P + P], att[:, 4 * q + t, c * P:c * P + P], C.ident[:, :])
                        last.then_inc(oT_made, 1)
                    for j in range(2):
                        n = 4 * bt + 2 * q + j
                        pe.wait_ge(attT_ready, 4 * bt + 2 * q + 2)
                        if n >= 1:
                            pe.wait_ge(y_ready, n)
                        for t in range(2):
                            for c in range(DC):
                                last = nc.tensor.matmul(y_ps[:, t * D:t * D + D], attT[:, c, (2 * j + t) * P:(2 * j + t) * P + P], w_o[:, c, :],
                                                        start=(c == 0), stop=(c == DC - 1))
                        last.then_inc(y_made, 1)

            project(0)
            for bt in range(NBT):
                if bt + 1 < NBT:
                    project(bt + 1)
                finish(bt)

        @block.scalar
        def _(act):
            def read_xT(bt):
                for n in range(4):
                    c, q = n % 2, n // 2
                    act.wait_ge(tr_made, 4 * bt + n + 1)
                    if bt >= 1:
                        act.wait_ge(b_made, NTM * bt)
                    nc.scalar.activation(xnT[:, c, 4 * q * P:4 * q * P + 4 * P], tr_ps[n % 2][:, :], ACT.Copy).then_inc(xnT_ready, 1)

            read_xT(0)
            for bt in range(NBT):
                if bt + 1 < NBT:
                    read_xT(bt + 1)
                for q in range(2):
                    act.wait_ge(shifted, 2 * bt + q + 1)
                    if bt >= 1:
                        act.wait_ge(summed, 2 * NTM * bt)
                    nc.scalar.activation(weight[:, 4 * q:4 * q + 4, :, :], score[:, 4 * q:4 * q + 4, :, :], ACT.Exp, scale=SCALE).then_inc(weights_ready, 1)
                for q in range(2):
                    for c in range(DC):
                        act.wait_ge(oT_made, 4 * bt + 2 * q + c + 1)
                        if 4 * bt + 2 * q >= 2:
                            act.wait_ge(y_made, 4 * bt + 2 * q)
                        nc.scalar.activation(attT[:, c, :], oT_ps[:, :], ACT.Copy).then_inc(attT_ready, 1)

        @block.vector
        def _(dve):
            dve.wait_ge(params, NPARAM)
            dve.wait_ge(made, 3)
            for o in range(DC):
                nc.vector.tensor_scalar(bq_wide[:, o, :], C.ones[:, :], bq[:, o:o + 1], None, ALU.mult).then_inc(rel_made, 1)
            nc.vector.tensor_tensor(rel_heads[:, :, :, :], rel[:, :].unsqueeze(1).unsqueeze(3).to_broadcast([P, DC, NREL, H]),
                                    head[:, :, :].unsqueeze(2).to_broadcast([P, DC, NREL, H]), ALU.mult).then_inc(rel_made, 1)
            dve.wait_ge(rel_ps, 1)
            for c in range(DC):
                nc.vector.tensor_copy(w_rel[:, c, :], a_ps[c][:, 0:NREL * H])
            nc.vector.tensor_copy(b_rel[:, :], b_ps[0][:, 0:NREL * H]).then_inc(rel_ready, 1)
            dve.wait_ge(rel_ready, 1)

            def stats(bt):
                dve.wait_ge(x_loaded[bt % 3], 16 * (bt // 3 + 1))
                if bt >= 1:
                    dve.wait_ge(xn_ready, bt)
                for t in range(NTM):
                    last = nc.vector.bn_stats(st[:, t, :], x[bt % 3][:, t, :])
                last.then_inc(st_done, 1)
                dve.wait_ge(st_done, bt + 1)
                for t in range(NTM):
                    last = nc.vector.bn_aggr(mv[:, t, :], st[:, t, :])
                last.then_inc(mv_done, 1)

            def norm(bt):
                dve.wait_ge(rstd_done, bt + 1)
                if bt >= 1:
                    dve.wait_ge(tr_made, 4 * bt)
                for t in range(NTM):
                    last = nc.vector.tensor_scalar(xn[:, t, :], x[bt % 3][:, t, :], mv[:, t, 0:1], rstd[:, t:t + 1], ALU.subtract, ALU.mult)
                last.then_inc(xn_ready, 1)

            def read_projections(bt, t):
                n = NTM * bt + t
                i = bt % 2
                dve.wait_ge(a_made, n + 1)
                nc.vector.tensor_tensor(qkv[i][:, t, 0:2 * D], a_ps[t % 2][:, :], bias[:, 0:2 * D], ALU.add).then_inc(a_ready, 1)
                dve.wait_ge(b_made, n + 1)
                nc.vector.tensor_tensor(qkv[i][:, t, 2 * D:3 * D], b_ps[t % 2][:, 0:D], bias[:, 2 * D:3 * D], ALU.add)
                r0 = (NTM - 1 - t) * H
                nc.vector.tensor_tensor(q_rel[i][:, t, :], b_ps[t % 2][:, D:D + P], b_rel[:, r0:r0 + P], ALU.add).then_inc(b_ready, 1)

            def add_up(bt, n):
                m = 2 * NTM * bt + n
                t = n % NTM
                buf = prod[m % RING][:, :]
                if n in ON_DVE:
                    if m >= RING:
                        dve.wait_ge(summed, m - RING + 1)
                    dve.wait_ge(a_ready if n < NTM else weights_ready, NTM * (bt + 1) if n < NTM else 2 * bt + 2)
                    product(nc.vector, bt, n).then_inc(dve_prod, 1)
                    dve.wait_ge(dve_prod, n_dve * bt + ON_DVE.index(n) + 1)
                else:
                    dve.wait_ge(pool_prod, len(on_pool) * bt + on_pool.index(n) + 1)
                if n < NTM:
                    nc.vector.tensor_reduce(score[:, t, :, :], buf.rearrange("p (s h e) -> p s h e", s=NTM, h=H), AX.X, ALU.add).then_inc(summed, 1)
                else:
                    if n == NTM and bt >= 1:
                        dve.wait_ge(oT_made, 4 * bt)
                    nc.vector.tensor_reduce(att[:, t, :], buf.rearrange("p (s c) -> p c s", s=NTM), AX.X, ALU.add).then_inc(summed, 1)

            def shift(bt, q):
                ts = slice(4 * q, 4 * q + 4)
                s4 = score[:, ts, :, :]
                base = 2 * (2 * bt + q)
                dve.wait_ge(summed, 2 * NTM * bt + 4 * q + 4)
                nc.vector.tensor_tensor(s4, s4, q_rel[bt % 2][:, ts, :].rearrange("p t (s h) -> p t s h", s=NTM), ALU.add).then_inc(soft, 1)
                dve.wait_ge(soft, base + 1)
                nc.vector.tensor_reduce(peak[:, ts, :], s4.rearrange("p t s h -> p t h s"), AX.X, ALU.max).then_inc(soft, 1)
                dve.wait_ge(soft, base + 2)
                nc.vector.tensor_tensor(s4, s4, peak[:, ts, :].unsqueeze(2).to_broadcast([P, 4, NTM, H]), ALU.subtract).then_inc(shifted, 1)

            def total_weight(bt, q):
                ts = slice(4 * q, 4 * q + 4)
                dve.wait_ge(weights_ready, 2 * bt + q + 1)
                nc.vector.tensor_reduce(total[:, ts, :], weight[:, ts, :, :].rearrange("p t s h -> p t h s"), AX.X, ALU.add).then_inc(inv_step, 1)
                dve.wait_ge(inv_step, 2 * (2 * bt + q) + 1)
                nc.vector.reciprocal(inv[:, ts, :], total[:, ts, :]).then_inc(inv_step, 1)

            def normalise(bt, q):
                ts = slice(4 * q, 4 * q + 4)
                dve.wait_ge(summed, 2 * NTM * bt + NTM + 4 * q + 4)
                dve.wait_ge(inv_step, 2 * (2 * bt + q) + 2)
                a = att[:, ts, :].rearrange("p t (h e) -> p t h e", h=H)
                nc.vector.tensor_tensor(a, a, inv[:, ts, :].unsqueeze(3).to_broadcast([P, 4, H, HD]), ALU.mult).then_inc(normed, 1)

            def add_residual(bt, q):
                for j in range(2):
                    t = 4 * q + 2 * j
                    dve.wait_ge(y_made, 4 * bt + 2 * q + j + 1)
                    if bt >= 1:
                        dve.wait_ge(stored, 16 * bt)
                    dve.wait_ge(x_biased, bt + 1)
                    nc.vector.tensor_tensor(out[:, t:t + 2, :], y_ps[:, :].rearrange("p (t d) -> p t d", t=2), x[bt % 3][:, t:t + 2, :],
                                            ALU.add).then_inc(y_ready, 1)

            stats(0)
            norm(0)
            for t in range(NTM):
                read_projections(0, t)
            for bt in range(NBT):
                if bt + 1 < NBT:
                    stats(bt + 1)
                    norm(bt + 1)
                for t in range(NTM):
                    add_up(bt, t)
                    if bt >= 1 and t == 0:
                        add_residual(bt - 1, 1)
                    if t == 3:
                        shift(bt, 0)
                    if bt + 1 < NBT:
                        read_projections(bt + 1, t)
                shift(bt, 1)
                total_weight(bt, 0)
                for t in range(NTM):
                    add_up(bt, NTM + t)
                    if t == 1:
                        total_weight(bt, 1)
                    if t == 3:
                        normalise(bt, 0)
                normalise(bt, 1)
                add_residual(bt, 0)
            add_residual(NBT - 1, 1)

        @block.gpsimd
        def _(pool):
            pool.memset(half[:, :], -0.5)
            pool.memset(head[:, :, :], 1.0).then_inc(made, 1)
            pool.wait_ge(made, 1)
            pool.affine_select(out=head[:, :, :], in_=head[:, :, :], compare_op=ALU.is_ge, fill=0.0, base=0,
                               pattern=[[P, DC], [-HD, H]], channel_multiplier=1).then_inc(made, 1)
            pool.wait_ge(made, 2)
            pool.affine_select(out=head[:, :, :], in_=head[:, :, :], compare_op=ALU.is_ge, fill=0.0, base=HD - 1,
                               pattern=[[-P, DC], [HD, H]], channel_multiplier=-1).then_inc(made, 1)

            def inv_std(bt):
                pool.wait_ge(mv_done, bt + 1)
                nc.gpsimd.tensor_scalar(var[:, :], mv[:, :, 1], EPS, None, ALU.add).then_inc(var_done, 1)
                pool.wait_ge(var_done, bt + 1)
                nc.gpsimd.tensor_tensor(rstd[:, :], var[:, :], half[:, :], ALU.pow).then_inc(rstd_done, 1)
                pool.wait_ge(xn_ready, bt + 1)
                if bt == 0:
                    pool.wait_ge(params, NPARAM)
                nc.gpsimd.tensor_tensor(x[bt % 3][:, :, :], x[bt % 3][:, :, :], bias_o[:, :].unsqueeze(1).to_broadcast([P, NTM, D]),
                                        ALU.add).then_inc(x_biased, 1)

            inv_std(0)
            for bt in range(NBT):
                if bt + 1 < NBT:
                    inv_std(bt + 1)
                for n in on_pool:
                    m = 2 * NTM * bt + n
                    if m >= RING:
                        pool.wait_ge(summed, m - RING + 1)
                    if n == 0:
                        pool.wait_ge(a_ready, NTM * (bt + 1))
                    if n in (NTM, NTM + 4):
                        pool.wait_ge(b_ready, NTM * (bt + 1))
                        pool.wait_ge(weights_ready, 2 * bt + 1 + (n - NTM) // 4)
                    product(nc.gpsimd, bt, n).then_inc(pool_prod, 1)



def program(nc, A, out):
    with ExitStack() as ctx:
        S = semaphores(nc, ctx)
        C = constants(nc, ctx, S, A)
        dram = scratch(nc)
        expert_sems = {}
        x_d = [nc.dram_tensor(f"layer{n}_d", [NB, T, D], F32).ap() for n in (1, 2, 3)]
        x1_d = nc.dram_tensor("normed_d", [NB, T, D], F32).ap()
        with ExitStack() as layer:
            M = attention_memory(nc, layer, "a", dram)
            attention_preset(nc, M, S, 0)
            attention(nc, M, S, C, Layer(
                base=0, t_base=0, src_base=0, causal=True, ffn=False, x_src=A["x"], x_dst=x_d[0], w_qkv=C.wa_qkv,
                w_o=C.wa_o, b_qk=C.no_bias, b_v=None, b_o=None))

        def transformer(k, x_src, x_dst):
            with ExitStack() as layer:
                M = attention_memory(nc, layer, f"f{k}", dram)
                attention_preset(nc, M, S, 2 + 2 * k)
                attention(nc, M, S, C, Layer(
                    base=NB * (1 + k), t_base=NB * NG * (20 + 16 * k), src_base=NB * k, causal=False, ffn=True,
                    x_src=x_src, x_dst=x1_d, w_qkv=C.wf_qkv, w_o=C.wf_o, b_qk=C.b_qk, b_v=C.b_v, b_o=C.b_o))
            with ExitStack() as layer:
                experts(nc, expert_sems, layer, C, A, k, x_src, x1_d, x_dst)

        transformer(0, x_d[0], x_d[1])
        with ExitStack() as layer:
            local_attention(nc, layer, C, A, x_d[1], x_d[2])
        transformer(1, x_d[2], out)


_INS = {"x": "L0_attn_a_x", "a_w_qkv": "L0_attn_a_w_qkv", "a_w_proj": "L0_attn_a_w_proj",
        "b_w_in": "L0_attn_b_in_proj_weight", "b_b_in": "L0_attn_b_in_proj_bias", "b_w_nat": "L0_attn_b_in_proj_weight",
        "b_rel": "L0_attn_b_rel_pos_keys",
        "b_w_out": "L0_attn_b_out_w", "b_b_out": "L0_attn_b_out_b", "f_Wq": "L0_ffn_Wq", "f_bq": "L0_ffn_bq",
        "f_Wk": "L0_ffn_Wk", "f_bk": "L0_ffn_bk", "f_Wv": "L0_ffn_Wv", "f_bv": "L0_ffn_bv", "f_Wo": "L0_ffn_Wo",
        "f_bo": "L0_ffn_bo", "f_router_w": "L0_ffn_router_w", "f_router_b": "L0_ffn_router_b", "f_W1": "L0_ffn_W1",
        "f_b1": "L0_ffn_b1", "f_W2": "L0_ffn_W2", "f_b2": "L0_ffn_b2", "f_ln1_g": "L0_ffn_ln1_g",
        "f_ln1_b": "L0_ffn_ln1_b", "f_ln2_g": "L0_ffn_ln2_g", "f_ln2_b": "L0_ffn_ln2_b"}
_TRANSPOSED = ("a_w_qkv", "a_w_proj", "b_w_in", "b_w_out", "b_rel")


def kernel(**inputs):
    import numpy as _np
    import concourse.bacc as _bacc
    from concourse import mybir as _mybir
    from concourse.bass_utils import run_bass_kernel_spmd as _run

    nc = _bacc.Bacc("TRN2", target_bir_lowering=False, num_devices=1)
    arrays, args = {}, {}
    for short, name in _INS.items():
        a = _np.asarray(inputs[name])
        a = _np.ascontiguousarray(a.T if short in _TRANSPOSED else a)
        arrays[f"in_{short}_dram"] = a
        args[short] = nc.dram_tensor(f"in_{short}_dram", a.shape, _mybir.dt.from_np(a.dtype), kind="ExternalInput").ap()
    out = nc.dram_tensor("out_0_dram", (NB, T, D), _mybir.dt.float32, kind="ExternalOutput").ap()
    program(nc, args, out)
    r = _run(nc, [arrays], core_ids=[0])
    return r.results[0]["out_0_dram"]
```
